# Optimizing a Trainium2 kernel written in Bass

```python
import numpy as np
import jax
import jax.numpy as jnp

def _softmax(x, axis=-1):
    return jax.nn.softmax(x, axis=axis)

def _gelu(x):
    return jax.nn.gelu(x, approximate=True)

def _silu(x):
    return jax.nn.silu(x)

def _sigmoid(x):
    return jax.nn.sigmoid(x)

def _layernorm(x, axis=-1, eps=1e-05):
    m = jnp.mean(x, axis=axis, keepdims=True)
    v = jnp.var(x, axis=axis, keepdims=True)
    return (x - m) / jnp.sqrt(v + eps)

def _scatter_add(tgt, idx, src, axis=0):
    return tgt.at[idx].add(src)

def _segment_sum(src, seg, n):
    return jax.ops.segment_sum(src, seg, n)
kernel_name = 'mk_adaln_ffn_d1_seqx_r4_7a313b'

def setup_inputs(seed: int=0):
    np.random.seed(seed)
    _w = jnp.asarray

    def _rec_inputs():
        import jax
        import jax.numpy as jnp
        _rk = jax.random.key(seed)
        x = -0.000125 + 0.9999 * jax.random.normal(jax.random.fold_in(_rk, 1), (128, 64, 1024), jnp.float32)
        _lenS = 64 - jax.random.randint(jax.random.fold_in(_rk, 7), (128,), 0, max(1, 64 // 4) + 1, jnp.int32)
        _lenS2 = 64 - jax.random.randint(jax.random.fold_in(_rk, 8), (128,), 0, max(1, 64 // 4) + 1, jnp.int32)
        cond_128 = 0.0061147 + 1.02565 * jax.random.normal(jax.random.fold_in(_rk, 11), (128, 128), jnp.float32)
        fside_S_0 = -0.022604 + 0.987366 * jax.random.normal(jax.random.fold_in(_rk, 12), (64,), jnp.float32)
        return (x, cond_128, fside_S_0)
    x, cond_128, fside_S_0 = _rec_inputs()

    def _L0_cond_setup():
        import jax, jax.numpy as jnp
        import numpy as np
        from jax import lax
        N, C_IN, L = (32, 64, 1024)
        C_OUT, K, GROUPS = (64, 9, 4)
        C_DIM, PAD, STRIDE = (128, 4, 1)
        key = jax.random.key(seed)
        k1, k2, k3, k4, k5 = jax.random.split(key, 5)
        x = jax.random.normal(k1, (N, C_IN, L), dtype=jnp.float32)
        c = jax.random.normal(k2, (N, C_DIM), dtype=jnp.float32)
        weight = jax.random.normal(k3, (C_OUT, C_IN // GROUPS, K), dtype=jnp.float32)
        c_weight = jax.random.normal(k4, (C_OUT, C_DIM), dtype=jnp.float32)
        bias = jax.random.normal(k5, (C_OUT,), dtype=jnp.float32)
        return {'x': x, 'c': c, 'weight': weight, 'c_weight': c_weight, 'bias': bias}
    _L0_cond_all = _L0_cond_setup()
    _L0_cond_in = {k: v for k, v in _L0_cond_all.items() if k in ('weight', 'c_weight')}
    del _L0_cond_all

    def _L0_ffn_setup():
        import jax, jax.numpy as jnp
        import numpy as np
        N_EXPERTS = 28
        TOP_K = 2
        RANK = 8
        LORA_ALPHA = 16
        SCALING = LORA_ALPHA / RANK
        TEMP = 1.0
        key = jax.random.key(seed)
        ks = jax.random.split(key, 5)
        B, S, D_IN, D_OUT = (4, 512, 1024, 1024)
        x = jax.random.normal(ks[0], (B, S, D_IN), dtype=jnp.float32)
        base_W = jax.random.normal(ks[1], (D_OUT, D_IN), dtype=jnp.float32) * (1.0 / np.sqrt(D_IN))
        gate_W = jax.random.normal(ks[2], (N_EXPERTS, D_IN), dtype=jnp.float32) * (1.0 / np.sqrt(D_IN))
        lora_A = jax.random.normal(ks[3], (N_EXPERTS, RANK, D_IN), dtype=jnp.float32) * (1.0 / np.sqrt(D_IN))
        lora_B = jax.random.normal(ks[4], (N_EXPERTS, D_OUT, RANK), dtype=jnp.float32) * 0.01
        return {'x': x, 'base_W': base_W, 'gate_W': gate_W, 'lora_A': lora_A, 'lora_B': lora_B}
    _L0_ffn_all = _L0_ffn_setup()
    _L0_ffn_in = {k: v for k, v in _L0_ffn_all.items() if k in ('base_W', 'gate_W', 'lora_A', 'lora_B')}
    del _L0_ffn_all
    return {'x': x, 'cond_128': cond_128, 'fside_S_0': fside_S_0, 'L0_cond_weight': _L0_cond_in['weight'], 'L0_cond_c_weight': _L0_cond_in['c_weight'], 'L0_ffn_base_W': _L0_ffn_in['base_W'], 'L0_ffn_gate_W': _L0_ffn_in['gate_W'], 'L0_ffn_lora_A': _L0_ffn_in['lora_A'], 'L0_ffn_lora_B': _L0_ffn_in['lora_B']}

def reference(x, cond_128, fside_S_0, L0_cond_weight, L0_cond_c_weight, L0_ffn_base_W, L0_ffn_gate_W, L0_ffn_lora_A, L0_ffn_lora_B):
    import jax
    import jax.numpy as jnp

    def _L0_cond_ref(x, c, weight, c_weight, bias):
        import jax, jax.numpy as jnp
        import numpy as np
        from jax import lax
        N, C_IN, L = (32, 64, 1024)
        C_OUT, K, GROUPS = (64, 9, 4)
        C_DIM, PAD, STRIDE = (128, 4, 1)
        out = lax.conv_general_dilated(x, weight, window_strides=(STRIDE,), padding=[(PAD, PAD)], dimension_numbers=('NCH', 'OIH', 'NCH'), feature_group_count=GROUPS)
        ctx = jnp.einsum('nd,od->no', c, c_weight)
        out = out + ctx[:, :, None] + bias[None, :, None]
        return out

    def _L0_ffn_ref(x, base_W, gate_W, lora_A, lora_B):
        import jax, jax.numpy as jnp
        import numpy as np
        N_EXPERTS = 28
        TOP_K = 2
        RANK = 8
        LORA_ALPHA = 16
        SCALING = LORA_ALPHA / RANK
        TEMP = 1.0
        B, S, D_in = x.shape
        xf = x.reshape(B * S, D_in)
        base = xf @ base_W.T
        logits = xf @ gate_W.T
        top_vals, top_idx = jax.lax.top_k(logits, TOP_K)
        top_probs = jax.nn.softmax(top_vals / TEMP, axis=-1)
        N = xf.shape[0]
        gate_full = jnp.zeros((N, N_EXPERTS), dtype=xf.dtype).at[jnp.arange(N)[:, None], top_idx].add(top_probs)
        h = jnp.einsum('nd,erd->ner', xf, lora_A)
        h = h * (gate_full * SCALING)[:, :, None]
        lora_out = jnp.einsum('ner,eor->no', h, lora_B)
        out = base + lora_out
        return out.reshape(B, S, -1)
    x = x + _L0_ffn_ref(_L0_cond_ref(x, cond_128, L0_cond_weight, L0_cond_c_weight, fside_S_0), L0_ffn_base_W, L0_ffn_gate_W, L0_ffn_lora_A, L0_ffn_lora_B)
    return x

_drawn_inputs = setup_inputs


def setup_inputs(seed=0):
    import zlib

    import numpy as np

    out = dict(_drawn_inputs(seed))
    spreads = {}
    factors = {}
    for name, (base, spread) in spreads.items():
        noise = np.random.default_rng([zlib.crc32(name.encode()), seed]).standard_normal(out[name].shape)
        drawn = base * np.exp(spread * noise) if base else spread * noise
        out[name] = jnp.asarray(drawn.astype(out[name].dtype))
    for name, factor in factors.items():
        out[name] = (out[name] * factor).astype(out[name].dtype)
    return out
```

```python
from contextlib import ExitStack

import concourse.bass as bass
from concourse import mybir

F32 = mybir.dt.float32
F32R = mybir.dt.float32r
U32 = mybir.dt.uint32
ALU = mybir.AluOpType
ACT = mybir.ActivationFunctionType


P = 128
IMAGES = 128
CHANNELS = 64
LENGTH = 1024
GROUPS = 4
GC = CHANNELS // GROUPS
TAPS = 9
PAD = TAPS // 2
PH = P // GC
BLOCKS = LENGTH // PH
EXPERTS = 28
RANK = 8
HID = EXPERTS * RANK
SIDE = EXPERTS + HID
D_OUT = 1024
SCALING = 2.0
BANK = 512

CHUNK = 128
CHUNKS_PER_GROUP = LENGTH // CHUNK
CHUNK_BLOCKS = CHUNK // PH
XCOLS = CHUNK + PH
STEP_BLOCKS = BANK // P
STEPS = CHUNK_BLOCKS // STEP_BLOCKS
ROUNDS = STEPS + 1
HALF = HID // 2

TILES = CHANNELS
AHEAD = 10
PREP_ROUNDS = 4
GATE_STEPS = 8
W_ROUNDS = 2
W_CHUNKS = AHEAD


def adaln_ffn(nc, x, cond, fside, conv_w, cond_w, base_w, gate_w, lora_a, lora_b, out):
    y_dram = nc.dram_tensor("y_scratch", (CHANNELS, PH, BLOCKS, IMAGES), F32, kind="Internal").ap()
    bt_dram = nc.dram_tensor("lora_bt_scratch", (HID, D_OUT), F32, kind="Internal").ap()

    with ExitStack() as ctx:
        def sb(name, shape, dt=F32):
            return ctx.enter_context(nc.sbuf_tensor(name, shape, dt))

        def ps(name, shape):
            return ctx.enter_context(nc.psum_tensor(name, shape, F32))

        def sem(name):
            return ctx.enter_context(nc.semaphore(name))

        ident = sb("ident", [P, P])
        iota = sb("iota", [P, EXPERTS])
        wb_hi = sb("wb_hi", [P, PH, D_OUT], F32R)
        wb_lo = sb("wb_lo", [P, PH, D_OUT], F32R)
        ws_hi = sb("ws_hi", [P, PH, SIDE], F32R)
        ws_lo = sb("ws_lo", [P, PH, SIDE], F32R)
        bt_hi = sb("bt_hi", [HALF, 2, D_OUT], F32R)
        bt_lo = sb("bt_lo", [HALF, 2, D_OUT], F32R)
        toep_hi = sb("toep_hi", [P, GROUPS, 2 * P], F32R)
        toep_lo = sb("toep_lo", [P, GROUPS, 2 * P], F32R)
        zero_halo = sb("zero_halo", [P, GC, PAD])
        bias = sb("bias", [P, GROUPS, IMAGES])
        tc_hi = [sb(f"toep_cur_hi{i}", [P, 2, P], F32R) for i in range(2)]
        tc_lo = [sb(f"toep_cur_lo{i}", [P, 2, P], F32R) for i in range(2)]
        bias_cur = [sb(f"bias_cur{i}", [P, IMAGES]) for i in range(2)]
        xs = sb("x_chunk", [P, GC, XCOLS])
        xp = sb("x_packed", [P, CHUNK_BLOCKS + 1, P])
        xt_hi = sb("xt_hi", [P, CHUNK_BLOCKS + 1, IMAGES], F32R)
        xt_lo = sb("xt_lo", [P, CHUNK_BLOCKS + 1, IMAGES], F32R)
        y_st = sb("y_store", [P, STEPS, STEP_BLOCKS * IMAGES])
        y_raw = sb("y_raw", [P, 2, PH * IMAGES])
        yt_hi = [sb(f"yt_hi{i}", [P, PH, IMAGES], F32R) for i in range(2)]
        yt_lo = [sb(f"yt_lo{i}", [P, PH, IMAGES], F32R) for i in range(2)]
        res = sb("res", [P, 4, D_OUT])
        mx = sb("mx", [P, 8])
        mi = sb("mi", [P, 8], U32)
        mif = sb("mif", [P, 2])
        diff = sb("diff", [P, 1])
        ed = sb("ed", [P, 1])
        den = sb("den", [P, 1])
        p0 = sb("p0", [P, 1])
        is0 = sb("is0", [P, EXPERTS])
        is1 = sb("is1", [P, EXPERTS])
        gate = sb("gate", [P, EXPERTS])
        gh = sb("gh", [P, HID])
        gt_hi = sb("gt_hi", [HALF, 2, P], F32R)
        gt_lo = sb("gt_lo", [HALF, 2, P], F32R)

        ps_x = ps("ps_x", [P, BANK])
        ps_g = ps("ps_g", [P, BANK])
        ps_c = ps("ps_c", [P, BANK])
        ps_s = ps("ps_s", [P, BANK])
        ps_b = [ps(f"ps_b{i}", [P, 2, BANK]) for i in range(2)]
        w_bank = [ps_b[0][:, 0, :], ps_b[0][:, 1, :]]
        x_banks = [ps_x, ps_g]
        c_banks = [ps_c, ps_s]

        w_row = [res[:, i, :] for i in range(2)]
        lora_nat = y_raw[0:4 * EXPERTS, :, :].rearrange("p a n -> p (a n)")
        lora_dei = res[0:4 * EXPERTS, 2:4, :].rearrange("p a n -> p (a n)")
        lora_raw = y_raw[0:HALF, :, :].rearrange("p a n -> p (a n)")
        spread = y_st[0:CHANNELS, :, :].rearrange("p s (a h m) -> p (s a) h m", a=2, h=2)
        prep = sb("prep", [P, 5 * P])
        conv_nat = prep[0:CHANNELS, 0:GC * TAPS]
        cond_nat = prep[:, 160:160 + P]
        condw_nat = prep[0:CHANNELS, 288:288 + P]
        fside_nat = prep[0:1, 416:416 + CHANNELS]
        ones = prep[0:1, 480:480 + P]
        cond_t = y_raw[:, 1, 0:P]
        condw_rep = y_raw[:, 0, 0:CHANNELS * PH]
        fside_rep = y_raw[0:1, 1, P:P + CHANNELS * PH]

        x_in = sem("x_in")
        x_packed = sem("x_packed")
        w_in = [sem(f"w_in{i}") for i in range(2)]
        small_in = sem("small_in")
        lora_in = sem("lora_in")
        lora_out = sem("lora_out")
        lora_raw_in = sem("lora_raw_in")
        y_out = [sem(f"y_out{i}") for i in range(STEPS)]
        y_in = [sem(f"y_in{i}") for i in range(2)]
        res_in = [sem(f"res_in{i}") for i in range(4)]
        out_done = [sem(f"out_done{i}") for i in range(4)]
        const_ready = sem("const_ready")
        zero_ready = sem("zero_ready")
        passed = sem("passed")
        prep_step = sem("prep_step")
        spread_ready = sem("spread_ready")
        cond_ready = sem("cond_ready")
        bias_ready = sem("bias_ready")
        toep_made = sem("toep_made")
        toep_ready = sem("toep_ready")
        lora_split = sem("lora_split")
        lora_dei_ready = sem("lora_dei_ready")
        bt_hi_ready = sem("bt_hi_ready")
        bt_ready = sem("bt_ready")
        x_transposed = sem("x_transposed")
        x_hi = sem("x_hi")
        x_lo = sem("x_lo")
        w_transposed = sem("w_transposed")
        w_hi = sem("w_hi")
        w_lo = sem("w_lo")
        conv_done = sem("conv_done")
        y_evac = sem("y_evac")
        y_hi = sem("y_hi")
        y_lo = sem("y_lo")
        side_done = sem("side_done")
        gate_step = sem("gate_step")
        diff_ready = sem("diff_ready")
        exp_ready = sem("exp_ready")
        gh_ready = sem("gh_ready")
        g_transposed = sem("g_transposed")
        g_hi = sem("g_hi")
        g_lo = sem("g_lo")
        base_done = sem("base_done")
        out_ready = sem("out_ready")

        def wait(eng, s, value):
            if not isinstance(value, int) or value > 0:
                eng.wait_ge(s, value)

        def stand_alone(eng):
            eng.sem_inc(passed, 1)

        def x_round(u, par, k):
            return u * (2 * ROUNDS) + (PREP_ROUNDS + par * ROUNDS + k)

        def step_number(u, par, s):
            return u * (2 * STEPS) + (par * STEPS + s)

        def round_blocks(k):
            return range(k * STEP_BLOCKS, min((k + 1) * STEP_BLOCKS, CHUNK_BLOCKS + 1))

        def x_bank(par, k, both):
            return x_banks[(PREP_ROUNDS + par * ROUNDS + k) % 2] if both else ps_x

        def c_bank(s, both):
            return c_banks[s % 2] if both else ps_c

        def w_dest(u, par, half, hi):
            ph = slice(4 * half, 4 * half + 4)
            if isinstance(u, int) and 2 * u + par >= 8:
                wide, lo = (ws_hi if hi else ws_lo), par * (SIDE // 2)
                return wide[:, ph, lo:lo + SIDE // 2]
            wide = wb_hi if hi else wb_lo
            return wide[:, ph, bass.ds(u * (2 * P) + par * P, P)]

        def w_columns(u, par):
            return SIDE // 2 if isinstance(u, int) and 2 * u + par >= 8 else P

        def half_of(t):
            return ((0, 1, 2), (0, 1)) if t % 2 == 0 else ((3, 4), (2, 3))

        block = ctx.enter_context(nc.Block())

        @block.sync
        def _(sp):
            def load_x(u, par):
                group, pair = u // 4, u % 4
                if isinstance(u, int):
                    edge = pair == (0 if par == 0 else 3)
                    (load_x_edge if edge else load_x_inner)(u, group, pair, par)
                else:
                    group, pair = sp.snap(group), sp.snap(pair)
                    with sp.If(pair == (0 if par == 0 else 3)):
                        load_x_edge(u, group, pair, par)
                    with sp.Else():
                        load_x_inner(u, group, pair, par)

            def load_x_inner(u, group, pair, par):
                first = pair * (2 * CHUNK) + (par * CHUNK - PAD)
                if not isinstance(first, int):
                    first = first.with_bounds(min_val=0, max_val=LENGTH - XCOLS)
                wait(sp, x_packed, u * 4 + par * 2)
                for h in range(2):
                    src = x[:, bass.ds(group * GC + h * (GC // 2), GC // 2), bass.ds(first, XCOLS)]
                    sp.dma_start(xs[:, h * (GC // 2):(h + 1) * (GC // 2), :], src).then_inc(x_in, 16)

            def load_x_edge(u, group, pair, par):
                here = slice(PAD, XCOLS) if par == 0 else slice(0, XCOLS - PAD)
                pad = slice(0, PAD) if par == 0 else slice(XCOLS - PAD, XCOLS)
                first = 0 if par == 0 else LENGTH - CHUNK - PAD
                src = x[:, bass.ds(group * GC, GC), first:first + XCOLS - PAD]
                wait(sp, x_packed, u * 4 + par * 2)
                sp.dma_start(xs[:, :, here], src).then_inc(x_in, 16)
                sp.dma_start(xs[:, :, pad], zero_halo[:, :, :]).then_inc(x_in, 16)

            def load_w(u, par):
                if not (isinstance(u, int) and u == 0):
                    wait(sp, w_transposed, u * (2 * W_ROUNDS) + (par - 1) * W_ROUNDS)
                if isinstance(u, int) and 2 * u + par == 8:
                    n = SIDE // 2 - EXPERTS
                    sp.dma_start(w_row[0][0:EXPERTS, :], gate_w).then_inc(w_in[0], 16)
                    sp.dma_start(w_row[0][EXPERTS:SIDE // 2, :], lora_rows[0:n, :]).then_inc(w_in[0], 16)
                elif isinstance(u, int) and 2 * u + par == 9:
                    n = SIDE // 2 - EXPERTS
                    sp.dma_start(w_row[1][0:SIDE // 2, :], lora_rows[n:HID, :]).then_inc(w_in[1], 16)
                else:
                    sp.dma_start(w_row[par], base_w[bass.ds(u * (2 * P) + par * P, P), :]).then_inc(w_in[par], 16)

            def load_tile_y(u, q):
                if q == 0:
                    for s in range(STEPS):
                        wait(sp, y_out[s], (u // 4 + 1) * (16 * CHUNKS_PER_GROUP))
                wait(sp, y_lo, u * 4 + (q - 1))
                sp.dma_start(y_raw[:, q % 2, :].rearrange("b (t n) -> b t n", t=PH),
                             y_dram[u * 4 + q].rearrange("t b n -> b t n")).then_inc(y_in[q % 2], 16)

            def load_tile_x(u, q):
                if not (isinstance(u, int) and u == 0):
                    wait(sp, out_done[q], u * 16)
                sp.dma_start(res[:, q, :], x[:, u * 4 + q, :]).then_inc(res_in[q], 16)

            lora_rows = lora_a.rearrange("e r d -> (e r) d")
            sp.dma_start(conv_nat, conv_w.rearrange("o c k -> o (c k)")).then_inc(small_in, 16)
            sp.dma_start(cond_nat, cond).then_inc(small_in, 16)
            sp.dma_start(condw_nat, cond_w).then_inc(small_in, 16)
            sp.dma_start(fside_nat, fside.rearrange("(a n) -> a n", a=1)).then_inc(small_in, 16)
            sp.wait_ge(zero_ready, 1)
            load_x(0, 0)
            load_x(0, 1)
            load_w(0, 0)
            load_w(0, 1)
            sp.wait_ge(bias_ready, 1)
            for k in range(4):
                sp.dma_start(lora_nat[k * EXPERTS:(k + 1) * EXPERTS, :],
                             lora_b[:, k * 256:(k + 1) * 256, :].rearrange("e o r -> e (o r)")).then_inc(lora_in, 16)
            with sp.Fori(1, 4) as u:
                for par in range(2):
                    load_x(u, par)
                    load_w(u, par)
            for par in range(2):
                load_x(4, par)
                load_w(4, par)
            sp.wait_ge(lora_out, 64)
            sp.dma_start(lora_raw.rearrange("p (h d) -> p h d", h=2),
                         bt_dram.rearrange("(h p) d -> p h d", h=2)).then_inc(lora_raw_in, 16)

            sp.wait_ge(bt_ready, 1)
            sp.wait_ge(w_transposed, W_ROUNDS * W_CHUNKS)

            def four_tiles(u, conv):
                for q in range(4):
                    load_tile_y(u, q)
                    if conv and q % 2 == 0:
                        load_x(u + AHEAD // 2, q // 2)
                    load_tile_x(u, q)

            four_tiles(0, True)
            with sp.Fori(1, 11) as u:
                four_tiles(u, True)
            with sp.Fori(11, 16) as u:
                four_tiles(u, False)

        @block.gpsimd
        def _(pool):
            def current_group(u, par):
                if not (isinstance(u, int) and u == 0):
                    wait(pool, y_evac, step_number(u, par, 0) - STEPS)
                group = (u // 4) % GROUPS
                stand_alone(pool)
                pool.tensor_copy(tc_hi[par][:, :, :].rearrange("p a n -> p (a n)").bitcast(F32R),
                                 toep_hi[:, group, :].bitcast(F32)).then_inc(toep_ready, 1)
                pool.tensor_copy(tc_lo[par][:, :, :].rearrange("p a n -> p (a n)").bitcast(F32R),
                                 toep_lo[:, group, :].bitcast(F32)).then_inc(toep_ready, 1)
                pool.tensor_copy(bias_cur[par][:, :], bias[:, group, :]).then_inc(toep_ready, 1)

            def pack_x(u, par, half):
                first = isinstance(u, int) and u == 0 and par == 0
                if half == 0:
                    pool.wait_ge(x_in, u * 64 + (par * 32 + 32))
                if not first:
                    pool.wait_ge(x_transposed, x_round(u, par, 0) - ROUNDS + (ROUNDS if half else 2))
                stand_alone(pool)
                lo, hi = (0, 2 * STEP_BLOCKS) if half == 0 else (2 * STEP_BLOCKS, CHUNK_BLOCKS + 1)
                pool.tensor_copy(xp[:, lo:hi, :].rearrange("p b (c j) -> p b c j", j=PH),
                                 xs[:, :, lo * PH:hi * PH].rearrange("p c (b j) -> p b c j", j=PH)
                                 ).then_inc(x_packed, 1)

            def store_y(u, par, s):
                pool.wait_ge(y_evac, step_number(u, par, s) + 1)
                group = u // 4
                first = (u % 4) * (2 * CHUNK_BLOCKS) + (par * CHUNK_BLOCKS + s * STEP_BLOCKS)
                dst = y_dram[bass.ds(group * GC, GC), :, bass.ds(first, STEP_BLOCKS), :]
                pool.dma_start(dst.rearrange("o t b n -> (o t) (b n)"), y_st[:, s, :]).then_inc(y_out[s], 16)

            def store_out(u, q):
                pool.wait_ge(out_ready, u * 4 + (q + 1))
                pool.dma_start(out[:, u * 4 + q, :], res[:, q, :]).then_inc(out_done[q], 16)

            pool.memset(zero_halo[:, :, :], 0.0).then_inc(zero_ready, 1)
            pool.memset(spread, 0.0).then_inc(const_ready, 1)
            pool.memset(ident[:, :], 0.0).then_inc(const_ready, 1)
            pool.wait_ge(const_ready, 2)
            pool.affine_select(out=ident[:, :], in_=ident[:, :], compare_op=ALU.not_equal, fill=1.0,
                               base=0, pattern=[[-1, P]], channel_multiplier=1).then_inc(const_ready, 1)
            pool.memset(ones, 1.0).then_inc(const_ready, 1)
            pool.iota(iota[:, :], pattern=[[1, EXPERTS]], base=0, channel_multiplier=0,
                      allow_small_or_imprecise_dtypes=True).then_inc(const_ready, 1)

            pack_x(0, 0, 0)
            pack_x(0, 0, 1)
            pool.wait_ge(toep_made, 2)
            pool.wait_ge(bias_ready, 1)
            current_group(0, 0)

            def chunk_step(u, par, s, more=True):
                store_y(u, par, s)
                if not more:
                    return
                if s == 0:
                    pack_x(u + par, 1 - par, 0)
                if s == 1:
                    current_group(u + par, 1 - par)
                if s == 2:
                    pack_x(u + par, 1 - par, 1)

            for s in range(STEPS):
                chunk_step(0, 0, s)
            pool.wait_ge(lora_dei_ready, 1)
            for k in range(4):
                pool.dma_start(bt_dram.rearrange("(e r) (k o) -> k e r o", r=RANK, k=4)[k],
                               lora_dei[k * EXPERTS:(k + 1) * EXPERTS, :].rearrange("e (r o) -> e r o", r=RANK)
                               ).then_inc(lora_out, 16)
            for s in range(STEPS):
                chunk_step(0, 1, s)
            with pool.Fori(1, 4) as u:
                for par in range(2):
                    for s in range(STEPS):
                        chunk_step(u, par, s)
            for par in range(2):
                for s in range(STEPS):
                    chunk_step(4, par, s)

            def four_tiles(u, conv, first=False, last=False):
                for q in range(4):
                    if q > 0:
                        store_out(u, q - 1)
                    elif not first:
                        store_out(u - 1, 3)
                    if conv:
                        for s in half_of(q)[1]:
                            chunk_step(u + AHEAD // 2, q // 2, s, not (last and q >= 2))

            four_tiles(0, True, True)
            with pool.Fori(1, 10) as u:
                four_tiles(u, True)
            four_tiles(10, True, False, True)
            with pool.Fori(11, 16) as u:
                four_tiles(u, False)
            store_out(15, 3)
            for s in range(STEPS):
                pool.wait_ge(y_out[s], 16 * GROUPS * CHUNKS_PER_GROUP)
            for q in range(4):
                pool.wait_ge(out_done[q], 16 * TILES // 4)

        @block.tensor
        def _(pe):
            def transpose_x(u, par, k, both):
                if k % 2 == 0 and k < 4:
                    pe.wait_ge(x_packed, u * 4 + (par * 2 + k // 2 + 1))
                r = x_round(u, par, k)
                wait(pe, x_lo, r - 1 if both else r)
                bank = x_bank(par, k, both)
                for i, b in enumerate(round_blocks(k)):
                    last = nc.tensor.transpose(bank[:, i * P:(i + 1) * P],
                                               xp[:, b, :], ident[:, :])
                last.then_inc(x_transposed, 1)

            def convolve(u, par, s, both):
                if s == 0:
                    pe.wait_ge(toep_ready, u * 6 + (par * 3 + 3))
                pe.wait_ge(x_lo, x_round(u, par, s + 1) + 1)
                n = step_number(u, par, s)
                wait(pe, y_evac, n - 1 if both else n)
                bank = c_bank(s, both)
                passes = [(w, v, h) for w, v in ((tc_lo, xt_hi), (tc_hi, xt_lo), (tc_hi, xt_hi)) for h in range(2)]
                for i, (w, v, h) in enumerate(passes):
                    b = s * STEP_BLOCKS + h
                    last = nc.tensor.matmul(bank[:, :], w[par][:, h, :], v[:, b:b + STEP_BLOCKS, :],
                                            start=(i == 0), stop=(i == len(passes) - 1))
                last.then_inc(conv_done, 1)

            def transpose_w(u, par, half):
                if half == 0:
                    if isinstance(u, int) and u == 4:
                        pe.wait_ge(w_in[par], 96 if par == 0 else 80)
                    else:
                        pe.wait_ge(w_in[par], u * 16 + 16)
                wait(pe, w_lo, u * 4 + (par * 2 + half - 1))
                rows = w_columns(u, par)
                for i in range(4):
                    ph = 4 * half + i
                    last = nc.tensor.transpose(w_bank[half][:, i * rows:(i + 1) * rows],
                                               w_row[par][0:rows, ph:D_OUT:PH], ident[0:rows, 0:rows])
                last.then_inc(w_transposed, 1)

            pe.wait_ge(small_in, 64)
            pe.wait_ge(const_ready, 5)
            nc.tensor.transpose(ps_x[:, 0:P], cond_nat, ident[:, :])
            nc.tensor.transpose(ps_x[:, P:P + CHANNELS], condw_nat,
                                ident[0:CHANNELS, 0:CHANNELS]).then_inc(x_transposed, 1)
            pe.wait_ge(spread_ready, 1)
            for h in range(2):
                if h == 1:
                    pe.wait_ge(x_lo, 1)
                bank = x_banks[1 - h]
                for t in range(PH):
                    last = nc.tensor.transpose(bank[:, t * CHANNELS:(t + 1) * CHANNELS],
                                               spread[:, t, h, :],
                                               ident[0:CHANNELS, 0:CHANNELS])
                last.then_inc(x_transposed, 1)
            pe.wait_ge(cond_ready, 1)
            pe.wait_ge(x_lo, 2)
            for g in range(GROUPS):
                nc.tensor.matmul(ps_g[:, g * P:(g + 1) * P], condw_rep[:, g * P:(g + 1) * P], cond_t,
                                 start=True, stop=False)
                last = nc.tensor.matmul(ps_g[:, g * P:(g + 1) * P], fside_rep[:, g * P:(g + 1) * P], ones,
                                        start=False, stop=True)
            last.then_inc(x_transposed, 1)

            def chunk(u, par):
                transpose_x(u, par, 0, True)
                transpose_x(u, par, 1, True)
                convolve(u, par, 0, True)
                transpose_x(u, par, 2, True)
                convolve(u, par, 1, True)
                transpose_w(u, par, 0)
                transpose_x(u, par, 3, True)
                convolve(u, par, 2, True)
                transpose_x(u, par, 4, True)
                transpose_w(u, par, 1)
                convolve(u, par, 3, True)

            chunk(0, 0)
            chunk(0, 1)
            with pe.Fori(1, 4) as u:
                for par in range(2):
                    chunk(u, par)
            chunk(4, 0)
            chunk(4, 1)

            def tile(u, q, conv):
                p = q % 2
                v, par = u + AHEAD // 2, q // 2
                rounds, steps = half_of(q)
                hi, lo = yt_hi[p], yt_lo[p]
                if conv:
                    transpose_x(v, par, rounds[0], False)
                pe.wait_ge(y_lo, u * 4 + (q + 1))
                wait(pe, gh_ready, u * 4 + q)
                for t in range(PH):
                    for i, (a, b) in enumerate(((hi, ws_lo), (lo, ws_hi), (hi, ws_hi))):
                        last = nc.tensor.matmul(ps_s[:, 0:SIDE], a[:, t, :], b[:, t, :],
                                                start=(t == 0 and i == 0), stop=(t == PH - 1 and i == 2))
                last.then_inc(side_done, 1)
                if conv:
                    transpose_x(v, par, rounds[1], False)
                wait(pe, out_ready, u * 4 + (q - 1))

                def base(phases):
                    for t in phases:
                        for i, (a, b) in enumerate(((hi, wb_lo), (lo, wb_hi), (hi, wb_hi))):
                            for h in range(2):
                                nc.tensor.matmul(ps_b[p][:, h, :], a[:, t, :], b[:, t, h * BANK:(h + 1) * BANK],
                                                 start=(t == 0 and i == 0), stop=False)

                base((0, 1))
                if conv:
                    convolve(v, par, steps[0], False)
                    if len(rounds) == 3:
                        transpose_x(v, par, rounds[2], False)
                base((2, 3))
                if conv:
                    convolve(v, par, steps[1], False)
                base((4, 5))
                pe.wait_ge(gh_ready, u * 4 + (q + 1))
                wait(pe, g_lo, u * 4 + q)
                for h in range(2):
                    last = nc.tensor.transpose(ps_g[0:HALF, h * P:(h + 1) * P], gh[:, h * HALF:(h + 1) * HALF],
                                               ident[:, :])
                last.then_inc(g_transposed, 1)
                base((6, 7))
                if isinstance(u, int) and u == 0 and q == 0:
                    pe.wait_ge(bt_ready, 1)
                pe.wait_ge(g_lo, u * 4 + (q + 1))
                for k in range(2):
                    for i, (a, b) in enumerate(((gt_hi, bt_lo), (gt_lo, bt_hi), (gt_hi, bt_hi))):
                        for h in range(2):
                            last = nc.tensor.matmul(ps_b[p][:, h, :], a[:, k, :], b[:, k, h * BANK:(h + 1) * BANK],
                                                    start=False, stop=(k == 1 and i == 2))
                last.then_inc(base_done, 1)

            pe.wait_ge(y_evac, AHEAD * STEPS)
            pe.wait_ge(w_lo, W_ROUNDS * W_CHUNKS)
            for q in range(4):
                tile(0, q, True)
            with pe.Fori(1, 11) as u:
                for q in range(4):
                    tile(u, q, True)
            with pe.Fori(11, 16) as u:
                for q in range(4):
                    tile(u, q, False)

        @block.scalar
        def _(act):
            def split_x(u, par, k, both):
                act.wait_ge(x_transposed, x_round(u, par, k) + 1)
                blocks = round_blocks(k)
                bank = x_bank(par, k, both)
                nc.scalar.activation(xt_hi[:, blocks.start:blocks.stop, :].rearrange("p b n -> p (b n)"),
                                     bank[:, 0:len(blocks) * P], ACT.Copy).then_inc(x_hi, 1)

            def split_w(u, par, half):
                act.wait_ge(w_transposed, u * 4 + (par * 2 + half + 1))
                rows = w_columns(u, par)
                nc.scalar.activation(w_dest(u, par, half, True),
                                     w_bank[half][:, 0:4 * rows].rearrange("p (t n) -> p t n", t=4),
                                     ACT.Copy).then_inc(w_hi, 1)

            def split_y(u, q):
                p = q % 2
                act.wait_ge(y_in[p], u * 32 + (16 * (q // 2) + 16))
                wait(act, base_done, u * 4 + (q - 1))
                nc.scalar.activation(yt_hi[p][:, :, :].rearrange("p t n -> p (t n)"), y_raw[:, p, :],
                                     ACT.Copy).then_inc(y_hi, 1)

            for h in range(2):
                act.wait_ge(x_transposed, h + 2)
                nc.scalar.activation(toep_hi[:, :, h * P:(h + 1) * P].rearrange("p g (o t) -> p g o t", t=PH),
                                     x_banks[1 - h][:, :].rearrange("p (t g o) -> p g o t", t=PH, g=GROUPS),
                                     ACT.Copy).then_inc(x_hi, 1)

            def chunk(u, par):
                split_x(u, par, 0, True)
                split_x(u, par, 1, True)
                split_x(u, par, 2, True)
                split_w(u, par, 0)
                split_x(u, par, 3, True)
                split_x(u, par, 4, True)
                split_w(u, par, 1)

            chunk(0, 0)
            act.wait_ge(lora_in, 64)
            act.wait_ge(toep_made, 2)
            nc.scalar.activation(lora_dei.rearrange("p (r o) -> p o r", r=RANK),
                                 lora_nat.rearrange("p (o r) -> p o r", r=RANK), ACT.Copy).then_inc(lora_dei_ready, 1)
            chunk(0, 1)
            with act.Fori(1, 4) as u:
                for par in range(2):
                    chunk(u, par)
            chunk(4, 0)
            chunk(4, 1)
            act.wait_ge(lora_raw_in, 16)
            nc.scalar.activation(bt_hi[:, :, :].rearrange("p h d -> p (h d)"), lora_raw,
                                 ACT.Copy).then_inc(bt_hi_ready, 1)

            def tile(u, q, conv, last=False):
                v, par = u + AHEAD // 2, q // 2
                rounds = half_of(q)[0]
                if conv:
                    split_x(v, par, rounds[0], False)
                    split_x(v, par, rounds[1], False)
                act.wait_ge(diff_ready, u * 4 + (q + 1))
                nc.scalar.activation(ed[:, :], diff[:, :], ACT.Exp).then_inc(exp_ready, 1)
                if conv and len(rounds) == 3:
                    split_x(v, par, rounds[2], False)
                if not last:
                    split_y(u + (1 if q == 3 else 0), (q + 1) % 4)
                act.wait_ge(g_transposed, u * 4 + (q + 1))
                nc.scalar.activation(gt_hi[:, :, :].rearrange("p h n -> p (h n)"), ps_g[0:HALF, 0:2 * P],
                                     ACT.Copy).then_inc(g_hi, 1)

            split_y(0, 0)
            for q in range(4):
                tile(0, q, True)
            with act.Fori(1, 11) as u:
                for q in range(4):
                    tile(u, q, True)
            with act.Fori(11, 15) as u:
                for q in range(4):
                    tile(u, q, False)
            for q in range(4):
                tile(15, q, False, q == 3)

        @block.vector
        def _(dve):
            def split_x(u, par, k, both):
                r = x_round(u, par, k)
                dve.wait_ge(x_hi, r - 1)
                blocks = round_blocks(k)
                bank = x_bank(par, k, both)
                cols = slice(blocks.start, blocks.stop)
                nc.vector.tensor_tensor(xt_lo[:, cols, :].rearrange("p b n -> p (b n)"),
                                        bank[:, 0:len(blocks) * P],
                                        xt_hi[:, cols, :].rearrange("p b n -> p (b n)").bitcast(F32),
                                        ALU.subtract).then_inc(x_lo, 1)

            def evacuate_conv(u, par, s, both):
                dve.wait_ge(conv_done, step_number(u, par, s) + 1)
                if s == 0:
                    dve.wait_ge(toep_ready, u * 6 + (par * 3 + 3))
                if not (isinstance(u, int) and u == 0 and par == 0):
                    wait(dve, y_out[s], u * 32 + par * 16)
                nc.vector.tensor_tensor(y_st[:, s, :].rearrange("p (b n) -> p b n", n=IMAGES),
                                        c_bank(s, both)[:, :].rearrange("p (b n) -> p b n", n=IMAGES),
                                        bias_cur[par][:, :].unsqueeze(1).to_broadcast([P, STEP_BLOCKS, IMAGES]),
                                        ALU.add).then_inc(y_evac, 1)

            def split_w(u, par, half):
                dve.wait_ge(w_hi, u * 4 + (par * 2 + half + 1))
                rows = w_columns(u, par)
                nc.vector.tensor_tensor(w_dest(u, par, half, False),
                                        w_bank[half][:, 0:4 * rows].rearrange("p (t n) -> p t n", t=4),
                                        w_dest(u, par, half, True).bitcast(F32), ALU.subtract).then_inc(w_lo, 1)

            def split_y(u, q):
                p = q % 2
                dve.wait_ge(y_hi, u * 4 + (q + 1))
                nc.vector.tensor_tensor(yt_lo[p][:, :, :].rearrange("p t n -> p (t n)"), y_raw[:, p, :],
                                        yt_hi[p][:, :, :].rearrange("p t n -> p (t n)").bitcast(F32),
                                        ALU.subtract).then_inc(y_lo, 1)

            dve.wait_ge(small_in, 64)
            dve.wait_ge(const_ready, 5)
            for t in range(PH):
                taps = conv_nat.rearrange("o (c k) -> o c k", k=TAPS)
                near = spread[:, t, 0, :].rearrange("o (c j) -> o c j", j=PH)
                far = spread[:, t, 1, :].rearrange("o (c j) -> o c j", j=PH)
                nc.vector.tensor_copy(near[:, :, t:PH], taps[:, :, 0:PH - t])
                ins = nc.vector.tensor_copy(far[:, :, 0:t + 1], taps[:, :, PH - t:TAPS])
            ins.then_inc(spread_ready, 1)
            nc.vector.tensor_copy(fside_rep.rearrange("p (o t) -> p o t", t=PH),
                                  fside_nat.unsqueeze(2).to_broadcast([1, CHANNELS, PH]))
            dve.wait_ge(x_transposed, 1)
            nc.vector.tensor_copy(cond_t, ps_x[:, 0:P])
            nc.vector.tensor_copy(condw_rep.rearrange("p (o t) -> p o t", t=PH),
                                  ps_x[:, P:P + CHANNELS].unsqueeze(2).to_broadcast([P, CHANNELS, PH])
                                  ).then_inc(x_lo, 1)
            nc.vector.engine_nop().then_inc(cond_ready, 1)
            for h in range(2):
                dve.wait_ge(x_hi, h + 1)
                cols = toep_hi[:, :, h * P:(h + 1) * P].rearrange("p g (o t) -> p g o t", t=PH)
                nc.vector.tensor_tensor(toep_lo[:, :, h * P:(h + 1) * P].rearrange("p g (o t) -> p g o t", t=PH),
                                        x_banks[1 - h][:, :].rearrange("p (t g o) -> p g o t", t=PH, g=GROUPS),
                                        cols.bitcast(F32), ALU.subtract).then_inc(x_lo, 1)
            nc.vector.engine_nop().then_inc(toep_made, 2)
            dve.wait_ge(x_transposed, PREP_ROUNDS)
            nc.vector.tensor_copy(bias[:, :, :].rearrange("p g n -> p (g n)"), ps_g[:, :]).then_inc(x_lo, 1)
            nc.vector.engine_nop().then_inc(bias_ready, 1)

            def chunk(u, par):
                split_x(u, par, 0, True)
                split_x(u, par, 1, True)
                split_x(u, par, 2, True)
                evacuate_conv(u, par, 0, True)
                split_w(u, par, 0)
                split_x(u, par, 3, True)
                evacuate_conv(u, par, 1, True)
                split_x(u, par, 4, True)
                split_w(u, par, 1)
                evacuate_conv(u, par, 2, True)
                evacuate_conv(u, par, 3, True)

            chunk(0, 0)
            chunk(0, 1)
            with dve.Fori(1, 4) as u:
                for par in range(2):
                    chunk(u, par)
            chunk(4, 0)
            chunk(4, 1)
            dve.wait_ge(bt_hi_ready, 1)
            nc.vector.tensor_tensor(bt_lo[:, :, :].rearrange("p h d -> p (h d)"), lora_raw,
                                    bt_hi[:, :, :].rearrange("p h d -> p (h d)").bitcast(F32),
                                    ALU.subtract).then_inc(bt_ready, 1)

            def add_residual(u, q):
                dve.wait_ge(base_done, u * 4 + (q + 1))
                dve.wait_ge(res_in[q], u * 16 + 16)
                nc.vector.tensor_tensor(res[:, q, :].rearrange("p (h d) -> p h d", h=2), ps_b[q % 2][:, :, :],
                                        res[:, q, :].rearrange("p (h d) -> p h d", h=2),
                                        ALU.add).then_inc(out_ready, 1)

            def tile(u, q, conv, first=False, last=False):
                v, par = u + AHEAD // 2, q // 2
                rounds, steps = half_of(q)
                at = (u * 4 + q) * GATE_STEPS
                if conv:
                    split_x(v, par, rounds[0], False)
                if q > 0:
                    add_residual(u, q - 1)
                elif not first:
                    add_residual(u - 1, 3)
                dve.wait_ge(side_done, u * 4 + (q + 1))
                stand_alone(dve)
                nc.vector.max(mx[:, :], ps_s[:, 0:EXPERTS]).then_inc(gate_step, 1)
                dve.wait_ge(gate_step, at + 1)
                nc.vector.tensor_tensor(diff[:, :], mx[:, 1:2], mx[:, 0:1], ALU.subtract).then_inc(diff_ready, 1)
                nc.vector.max_index(mi[:, :], mx[:, :], ps_s[:, 0:EXPERTS]).then_inc(gate_step, 1)
                dve.wait_ge(gate_step, at + 2)
                nc.vector.tensor_copy(mif[:, :], mi[:, 0:2]).then_inc(gate_step, 1)
                if conv:
                    split_x(v, par, rounds[1], False)
                dve.wait_ge(gate_step, at + 3)
                nc.vector.tensor_scalar(is0[:, :], iota[:, :], mif[:, 0:1], None, ALU.is_equal).then_inc(gate_step, 1)
                nc.vector.tensor_scalar(is1[:, :], iota[:, :], mif[:, 1:2], None, ALU.is_equal).then_inc(gate_step, 1)
                dve.wait_ge(exp_ready, u * 4 + (q + 1))
                nc.vector.tensor_scalar(den[:, :], ed[:, :], 1.0, 1.0 / SCALING, ALU.add, ALU.mult
                                        ).then_inc(gate_step, 1)
                dve.wait_ge(gate_step, at + 6)
                nc.vector.reciprocal(p0[:, :], den[:, :]).then_inc(gate_step, 1)
                nc.vector.scalar_tensor_tensor(out=gate[:, :], in0=is1[:, :], scalar=ed[:, 0:1], in1=is0[:, :],
                                               op0=ALU.mult, op1=ALU.add).then_inc(gate_step, 1)
                dve.wait_ge(gate_step, at + 8)
                wait(dve, g_transposed, u * 4 + q)
                nc.vector.scalar_tensor_tensor(
                    out=gh[:, :].rearrange("p (e r) -> p e r", r=RANK),
                    in0=ps_s[:, EXPERTS:SIDE].rearrange("p (e r) -> p e r", r=RANK), scalar=p0[:, 0:1],
                    in1=gate[:, :].unsqueeze(2).to_broadcast([P, EXPERTS, RANK]),
                    op0=ALU.mult, op1=ALU.mult).then_inc(gh_ready, 1)
                if conv:
                    evacuate_conv(v, par, steps[0], False)
                    if len(rounds) == 3:
                        split_x(v, par, rounds[2], False)
                if not last:
                    split_y(u + (1 if q == 3 else 0), (q + 1) % 4)
                if conv:
                    evacuate_conv(v, par, steps[1], False)
                dve.wait_ge(g_hi, u * 4 + (q + 1))
                nc.vector.tensor_tensor(gt_lo[:, :, :].rearrange("p h n -> p (h n)"), ps_g[0:HALF, 0:2 * P],
                                        gt_hi[:, :, :].rearrange("p h n -> p (h n)").bitcast(F32),
                                        ALU.subtract).then_inc(g_lo, 1)

            split_y(0, 0)
            for q in range(4):
                tile(0, q, True, q == 0)
            with dve.Fori(1, 11) as u:
                for q in range(4):
                    tile(u, q, True)
            with dve.Fori(11, 15) as u:
                for q in range(4):
                    tile(u, q, False)
            for q in range(4):
                tile(15, q, False, False, q == 3)
            add_residual(15, 3)


_INS = ["x", "cond_128", "fside_S_0", "L0_cond_weight", "L0_cond_c_weight", "L0_ffn_base_W", "L0_ffn_gate_W",
        "L0_ffn_lora_A", "L0_ffn_lora_B"]


def kernel(**inputs):
    import numpy as _np
    import concourse.bacc as _bacc
    from concourse.bass_utils import run_bass_kernel_spmd as _run

    nc = _bacc.Bacc("TRN2", target_bir_lowering=False, num_devices=1)
    arrays, args = {}, []
    for name in _INS:
        a = _np.ascontiguousarray(inputs[name])
        arrays[f"in_{name}"] = a
        args.append(nc.dram_tensor(f"in_{name}", a.shape, F32, kind="ExternalInput").ap())
    o = nc.dram_tensor("out_dram", (IMAGES, CHANNELS, D_OUT), F32, kind="ExternalOutput").ap()
    adaln_ffn(nc, *args, o)
    r = _run(nc, [arrays], core_ids=[0])
    return r.results[0]["out_dram"]
```

```python
from contextlib import ExitStack

import concourse.bass as bass
from concourse import mybir

F32 = mybir.dt.float32
F32R = mybir.dt.float32r
U32 = mybir.dt.uint32
ALU = mybir.AluOpType
ACT = mybir.ActivationFunctionType


P = 128
IMAGES = 128
CHANNELS = 64
LENGTH = 1024
GROUPS = 4
GC = CHANNELS // GROUPS
TAPS = 9
PAD = TAPS // 2
PH = P // GC
BLOCKS = LENGTH // PH
EXPERTS = 28
RANK = 8
HID = EXPERTS * RANK
SIDE = EXPERTS + HID
D_OUT = 1024
SCALING = 2.0
BANK = 512

CHUNK = 128
CHUNKS_PER_GROUP = LENGTH // CHUNK
CHUNK_BLOCKS = CHUNK // PH
XCOLS = CHUNK + PH
STEP_BLOCKS = BANK // P
STEPS = CHUNK_BLOCKS // STEP_BLOCKS
ROUNDS = STEPS + 1
HALF = HID // 2

TILES = CHANNELS
AHEAD = 10
PREP_ROUNDS = 4
GATE_STEPS = 8
W_ROUNDS = 2
W_CHUNKS = AHEAD


def adaln_ffn(nc, x, cond, fside, conv_w, cond_w, base_w, gate_w, lora_a, lora_b, out):
    y_dram = nc.dram_tensor("y_scratch", (CHANNELS, PH, BLOCKS, IMAGES), F32, kind="Internal").ap()
    bt_dram = nc.dram_tensor("lora_bt_scratch", (HID, D_OUT), F32, kind="Internal").ap()

    with ExitStack() as ctx:
        def sb(name, shape, dt=F32):
            return ctx.enter_context(nc.sbuf_tensor(name, shape, dt))

        def ps(name, shape):
            return ctx.enter_context(nc.psum_tensor(name, shape, F32))

        def sem(name):
            return ctx.enter_context(nc.semaphore(name))

        ident = sb("ident", [P, P])
        iota = sb("iota", [P, EXPERTS])
        wb_hi = sb("wb_hi", [P, PH, D_OUT], F32R)
        wb_lo = sb("wb_lo", [P, PH, D_OUT], F32R)
        ws_hi = sb("ws_hi", [P, PH, SIDE], F32R)
        ws_lo = sb("ws_lo", [P, PH, SIDE], F32R)
        bt_hi = sb("bt_hi", [HALF, 2, D_OUT], F32R)
        bt_lo = sb("bt_lo", [HALF, 2, D_OUT], F32R)
        toep_hi = sb("toep_hi", [P, GROUPS, 2 * P], F32R)
        toep_lo = sb("toep_lo", [P, GROUPS, 2 * P], F32R)
        zero_halo = sb("zero_halo", [P, GC, PAD])
        bias = sb("bias", [P, GROUPS, IMAGES])
        tc_hi = [sb(f"toep_cur_hi{i}", [P, 2, P], F32R) for i in range(2)]
        tc_lo = [sb(f"toep_cur_lo{i}", [P, 2, P], F32R) for i in range(2)]
        bias_cur = [sb(f"bias_cur{i}", [P, IMAGES]) for i in range(2)]
        xs = [sb(f"x_chunk{i}", [P, GC, XCOLS]) for i in range(2)]
        xp = sb("x_packed", [P, CHUNK_BLOCKS + 1, P])
        xt_hi = sb("xt_hi", [P, CHUNK_BLOCKS + 1, IMAGES], F32R)
        xt_lo = sb("xt_lo", [P, CHUNK_BLOCKS + 1, IMAGES], F32R)
        y_st = sb("y_store", [P, STEPS, STEP_BLOCKS * IMAGES])
        y_raw = sb("y_raw", [P, 2, PH * IMAGES])
        yt_hi = [sb(f"yt_hi{i}", [P, PH, IMAGES], F32R) for i in range(2)]
        yt_lo = [sb(f"yt_lo{i}", [P, PH, IMAGES], F32R) for i in range(2)]
        res = sb("res", [P, 4, D_OUT])
        mx = sb("mx", [P, 8])
        mi = sb("mi", [P, 8], U32)
        mif = sb("mif", [P, 2])
        diff = sb("diff", [P, 1])
        ed = sb("ed", [P, 1])
        den = sb("den", [P, 1])
        p0 = sb("p0", [P, 1])
        is0 = sb("is0", [P, EXPERTS])
        is1 = sb("is1", [P, EXPERTS])
        gate = sb("gate", [P, EXPERTS])
        gh = sb("gh", [P, HID])
        gt_hi = sb("gt_hi", [HALF, 2, P], F32R)
        gt_lo = sb("gt_lo", [HALF, 2, P], F32R)

        ps_x = ps("ps_x", [P, BANK])
        ps_g = ps("ps_g", [P, BANK])
        ps_c = ps("ps_c", [P, BANK])
        ps_s = ps("ps_s", [P, BANK])
        ps_b = [ps(f"ps_b{i}", [P, 2, BANK]) for i in range(2)]
        w_bank = [ps_b[0][:, 0, :], ps_b[0][:, 1, :]]
        x_banks = [ps_x, ps_g]
        c_banks = [ps_c, ps_s]

        w_row = [res[:, i, :] for i in range(2)]
        lora_nat = y_raw[0:4 * EXPERTS, :, :].rearrange("p a n -> p (a n)")
        lora_dei = res[0:4 * EXPERTS, 2:4, :].rearrange("p a n -> p (a n)")
        lora_raw = y_raw[0:HALF, :, :].rearrange("p a n -> p (a n)")
        spread = y_st[0:CHANNELS, :, :].rearrange("p s (a h m) -> p (s a) h m", a=2, h=2)
        prep = res[:, 2, :]
        conv_nat = prep[0:CHANNELS, 0:GC * TAPS]
        cond_nat = prep[:, 160:160 + P]
        condw_nat = prep[0:CHANNELS, 288:288 + P]
        fside_nat = prep[0:1, 416:416 + CHANNELS]
        ones = prep[0:1, 480:480 + P]
        cond_t = y_raw[:, 1, 0:P]
        condw_rep = y_raw[:, 0, 0:CHANNELS * PH]
        fside_rep = y_raw[0:1, 1, P:P + CHANNELS * PH]

        x_in = [sem(f"x_in{i}") for i in range(2)]
        x_packed = [sem(f"x_packed{i}") for i in range(2)]
        w_in = [sem(f"w_in{i}") for i in range(2)]
        small_in = sem("small_in")
        lora_in = sem("lora_in")
        lora_out = sem("lora_out")
        lora_raw_in = sem("lora_raw_in")
        y_out = [sem(f"y_out{i}") for i in range(STEPS)]
        y_in = [sem(f"y_in{i}") for i in range(2)]
        res_in = [sem(f"res_in{i}") for i in range(4)]
        out_done = [sem(f"out_done{i}") for i in range(4)]
        const_ready = sem("const_ready")
        zero_ready = sem("zero_ready")
        passed = sem("passed")
        prep_step = sem("prep_step")
        spread_ready = sem("spread_ready")
        cond_ready = sem("cond_ready")
        bias_ready = sem("bias_ready")
        toep_made = sem("toep_made")
        toep_ready = sem("toep_ready")
        lora_split = sem("lora_split")
        lora_dei_ready = sem("lora_dei_ready")
        bt_hi_ready = sem("bt_hi_ready")
        bt_ready = sem("bt_ready")
        x_transposed = sem("x_transposed")
        x_hi = sem("x_hi")
        x_lo = sem("x_lo")
        w_transposed = sem("w_transposed")
        w_hi = sem("w_hi")
        w_lo = sem("w_lo")
        conv_done = sem("conv_done")
        y_evac = sem("y_evac")
        y_hi = sem("y_hi")
        y_lo = sem("y_lo")
        side_done = sem("side_done")
        gate_step = sem("gate_step")
        diff_ready = sem("diff_ready")
        exp_ready = sem("exp_ready")
        gh_ready = sem("gh_ready")
        g_transposed = sem("g_transposed")
        g_hi = sem("g_hi")
        g_lo = sem("g_lo")
        base_done = sem("base_done")
        out_ready = sem("out_ready")

        def wait(eng, s, value):
            if not isinstance(value, int) or value > 0:
                eng.wait_ge(s, value)

        def stand_alone(eng):
            eng.sem_inc(passed, 1)

        def x_round(u, par, k):
            return u * (2 * ROUNDS) + (PREP_ROUNDS + par * ROUNDS + k)

        def step_number(u, par, s):
            return u * (2 * STEPS) + (par * STEPS + s)

        def round_blocks(k):
            return range(k * STEP_BLOCKS, min((k + 1) * STEP_BLOCKS, CHUNK_BLOCKS + 1))

        def x_bank(par, k, both):
            return x_banks[(PREP_ROUNDS + par * ROUNDS + k) % 2] if both else ps_x

        def c_bank(s, both):
            return c_banks[s % 2] if both else ps_c

        def w_dest(u, par, half, hi):
            ph = slice(4 * half, 4 * half + 4)
            if isinstance(u, int) and 2 * u + par >= 8:
                wide, lo = (ws_hi if hi else ws_lo), par * (SIDE // 2)
                return wide[:, ph, lo:lo + SIDE // 2]
            wide = wb_hi if hi else wb_lo
            return wide[:, ph, bass.ds(u * (2 * P) + par * P, P)]

        def w_columns(u, par):
            return SIDE // 2 if isinstance(u, int) and 2 * u + par >= 8 else P

        def half_of(t):
            return ((0, 1, 2), (0, 1)) if t % 2 == 0 else ((3, 4), (2, 3))

        block = ctx.enter_context(nc.Block())

        @block.sync
        def _(sp):
            def load_x(u, par):
                group, pair = u // 4, u % 4
                if isinstance(u, int):
                    edge = pair == (0 if par == 0 else 3)
                    (load_x_edge if edge else load_x_inner)(u, group, pair, par)
                else:
                    group, pair = sp.snap(group), sp.snap(pair)
                    with sp.If(pair == (0 if par == 0 else 3)):
                        load_x_edge(u, group, pair, par)
                    with sp.Else():
                        load_x_inner(u, group, pair, par)

            def load_x_inner(u, group, pair, par):
                first = pair * (2 * CHUNK) + (par * CHUNK - PAD)
                if not isinstance(first, int):
                    first = first.with_bounds(min_val=0, max_val=LENGTH - XCOLS)
                if not (isinstance(u, int) and u == 0):
                    for half in range(2):
                        wait(sp, x_packed[half], u * 2 + (par - 1))
                for h in range(2):
                    src = x[:, bass.ds(group * GC + h * (GC // 2), GC // 2), bass.ds(first, XCOLS)]
                    sp.dma_start(xs[par][:, h * (GC // 2):(h + 1) * (GC // 2), :], src).then_inc(x_in[par], 16)

            def load_x_edge(u, group, pair, par):
                here = slice(PAD, XCOLS) if par == 0 else slice(0, XCOLS - PAD)
                pad = slice(0, PAD) if par == 0 else slice(XCOLS - PAD, XCOLS)
                first = 0 if par == 0 else LENGTH - CHUNK - PAD
                src = x[:, bass.ds(group * GC, GC), first:first + XCOLS - PAD]
                if not (isinstance(u, int) and u == 0):
                    for half in range(2):
                        wait(sp, x_packed[half], u * 2 + (par - 1))
                sp.dma_start(xs[par][:, :, here], src).then_inc(x_in[par], 16)
                sp.dma_start(xs[par][:, :, pad], zero_halo[:, :, :]).then_inc(x_in[par], 16)

            def load_w(u, par):
                if not (isinstance(u, int) and u == 0):
                    wait(sp, w_transposed, u * (2 * W_ROUNDS) + (par - 1) * W_ROUNDS)
                if isinstance(u, int) and 2 * u + par == 8:
                    n = SIDE // 2 - EXPERTS
                    sp.dma_start(w_row[0][0:EXPERTS, :], gate_w).then_inc(w_in[0], 16)
                    sp.dma_start(w_row[0][EXPERTS:SIDE // 2, :], lora_rows[0:n, :]).then_inc(w_in[0], 16)
                elif isinstance(u, int) and 2 * u + par == 9:
                    n = SIDE // 2 - EXPERTS
                    sp.dma_start(w_row[1][0:SIDE // 2, :], lora_rows[n:HID, :]).then_inc(w_in[1], 16)
                else:
                    sp.dma_start(w_row[par], base_w[bass.ds(u * (2 * P) + par * P, P), :]).then_inc(w_in[par], 16)

            def load_tile_y(u, q):
                if q == 0:
                    for s in range(STEPS):
                        wait(sp, y_out[s], (u // 4 + 1) * (16 * CHUNKS_PER_GROUP))
                wait(sp, y_lo, u * 4 + (q - 1))
                sp.dma_start(y_raw[:, q % 2, :].rearrange("b (t n) -> b t n", t=PH),
                             y_dram[u * 4 + q].rearrange("t b n -> b t n")).then_inc(y_in[q % 2], 16)

            def load_tile_x(u, q):
                if not (isinstance(u, int) and u == 0):
                    wait(sp, out_done[q], u * 16)
                sp.dma_start(res[:, q, :], x[:, u * 4 + q, :]).then_inc(res_in[q], 16)

            lora_rows = lora_a.rearrange("e r d -> (e r) d")
            sp.dma_start(conv_nat, conv_w.rearrange("o c k -> o (c k)")).then_inc(small_in, 16)
            sp.dma_start(cond_nat, cond).then_inc(small_in, 16)
            sp.dma_start(condw_nat, cond_w).then_inc(small_in, 16)
            sp.dma_start(fside_nat, fside.rearrange("(a n) -> a n", a=1)).then_inc(small_in, 16)
            sp.wait_ge(zero_ready, 1)
            load_x(0, 0)
            load_x(0, 1)
            load_w(0, 0)
            load_w(0, 1)
            sp.wait_ge(bias_ready, 1)
            for k in range(4):
                sp.dma_start(lora_nat[k * EXPERTS:(k + 1) * EXPERTS, :],
                             lora_b[:, k * 256:(k + 1) * 256, :].rearrange("e o r -> e (o r)")).then_inc(lora_in, 16)
            with sp.Fori(1, 4) as u:
                for par in range(2):
                    load_x(u, par)
                    load_w(u, par)
            for par in range(2):
                load_x(4, par)
                load_w(4, par)
            load_x(AHEAD // 2, 0)
            sp.wait_ge(lora_out, 64)
            sp.dma_start(lora_raw.rearrange("p (h d) -> p h d", h=2),
                         bt_dram.rearrange("(h p) d -> p h d", h=2)).then_inc(lora_raw_in, 16)

            sp.wait_ge(bt_ready, 1)
            sp.wait_ge(w_transposed, W_ROUNDS * W_CHUNKS)

            def four_tiles(u, chunks):
                for q in range(4):
                    load_tile_y(u, q)
                    if q % 2 == 0 and q // 2 < chunks:
                        load_x(u + AHEAD // 2 + q // 2, 1 - q // 2)
                    load_tile_x(u, q)

            four_tiles(0, 2)
            with sp.Fori(1, 10) as u:
                four_tiles(u, 2)
            four_tiles(10, 1)
            with sp.Fori(11, 16) as u:
                four_tiles(u, 0)

        @block.gpsimd
        def _(pool):
            def current_group(u, par):
                if not (isinstance(u, int) and u == 0):
                    wait(pool, y_evac, step_number(u, par, 0) - STEPS)
                group = u // 4
                stand_alone(pool)
                pool.tensor_copy(tc_hi[par][:, :, :].rearrange("p a n -> p (a n)").bitcast(F32R),
                                 toep_hi[:, group, :].bitcast(F32)).then_inc(toep_ready, 1)
                pool.tensor_copy(tc_lo[par][:, :, :].rearrange("p a n -> p (a n)").bitcast(F32R),
                                 toep_lo[:, group, :].bitcast(F32)).then_inc(toep_ready, 1)
                pool.tensor_copy(bias_cur[par][:, :], bias[:, group, :]).then_inc(toep_ready, 1)

            pool.memset(zero_halo[:, :, :], 0.0).then_inc(zero_ready, 1)
            pool.memset(spread, 0.0).then_inc(const_ready, 1)
            pool.memset(ident[:, :], 0.0).then_inc(const_ready, 1)
            pool.wait_ge(const_ready, 2)
            pool.affine_select(out=ident[:, :], in_=ident[:, :], compare_op=ALU.not_equal, fill=1.0,
                               base=0, pattern=[[-1, P]], channel_multiplier=1).then_inc(const_ready, 1)
            pool.memset(ones, 1.0).then_inc(const_ready, 1)
            pool.iota(iota[:, :], pattern=[[1, EXPERTS]], base=0, channel_multiplier=0,
                      allow_small_or_imprecise_dtypes=True).then_inc(const_ready, 1)

            pool.wait_ge(toep_made, 2)
            pool.wait_ge(bias_ready, 1)
            current_group(0, 0)
            current_group(0, 1)
            pool.wait_ge(lora_dei_ready, 1)
            for k in range(4):
                pool.dma_start(bt_dram.rearrange("(e r) (k o) -> k e r o", r=RANK, k=4)[k],
                               lora_dei[k * EXPERTS:(k + 1) * EXPERTS, :].rearrange("e (r o) -> e r o", r=RANK)
                               ).then_inc(lora_out, 16)
            with pool.Fori(1, GROUPS * CHUNKS_PER_GROUP // 2) as u:
                for par in range(2):
                    current_group(u, par)

        @block.tensor
        def _(pe):
            def transpose_x(u, par, k, both):
                if k % 2 == 0 and k < 4:
                    pe.wait_ge(x_packed[k // 2], u * 2 + (par + 1))
                r = x_round(u, par, k)
                wait(pe, x_lo, r - 1 if both else r)
                bank = x_bank(par, k, both)
                for i, b in enumerate(round_blocks(k)):
                    last = nc.tensor.transpose(bank[:, i * P:(i + 1) * P],
                                               xp[:, b, :], ident[:, :])
                last.then_inc(x_transposed, 1)

            def convolve(u, par, s, both):
                if s == 0:
                    pe.wait_ge(toep_ready, u * 6 + (par * 3 + 3))
                pe.wait_ge(x_lo, x_round(u, par, s + 1) + 1)
                n = step_number(u, par, s)
                wait(pe, y_evac, n - 1 if both else n)
                bank = c_bank(s, both)
                passes = [(w, v, h) for w, v in ((tc_lo, xt_hi), (tc_hi, xt_lo), (tc_hi, xt_hi)) for h in range(2)]
                for i, (w, v, h) in enumerate(passes):
                    b = s * STEP_BLOCKS + h
                    last = nc.tensor.matmul(bank[:, :], w[par][:, h, :], v[:, b:b + STEP_BLOCKS, :],
                                            start=(i == 0), stop=(i == len(passes) - 1))
                last.then_inc(conv_done, 1)

            def transpose_w(u, par, half):
                if half == 0:
                    if isinstance(u, int) and u == 4:
                        pe.wait_ge(w_in[par], 96 if par == 0 else 80)
                    else:
                        pe.wait_ge(w_in[par], u * 16 + 16)
                wait(pe, w_lo, u * 4 + (par * 2 + half - 1))
                rows = w_columns(u, par)
                for i in range(4):
                    ph = 4 * half + i
                    last = nc.tensor.transpose(w_bank[half][:, i * rows:(i + 1) * rows],
                                               w_row[par][0:rows, ph:D_OUT:PH], ident[0:rows, 0:rows])
                last.then_inc(w_transposed, 1)

            pe.wait_ge(small_in, 64)
            pe.wait_ge(const_ready, 5)
            nc.tensor.transpose(ps_x[:, 0:P], cond_nat, ident[:, :])
            nc.tensor.transpose(ps_x[:, P:P + CHANNELS], condw_nat,
                                ident[0:CHANNELS, 0:CHANNELS]).then_inc(x_transposed, 1)
            pe.wait_ge(spread_ready, 1)
            for h in range(2):
                if h == 1:
                    pe.wait_ge(x_lo, 1)
                bank = x_banks[1 - h]
                for t in range(PH):
                    last = nc.tensor.transpose(bank[:, t * CHANNELS:(t + 1) * CHANNELS],
                                               spread[:, t, h, :],
                                               ident[0:CHANNELS, 0:CHANNELS])
                last.then_inc(x_transposed, 1)
            pe.wait_ge(cond_ready, 1)
            pe.wait_ge(x_lo, 2)
            for g in range(GROUPS):
                nc.tensor.matmul(ps_g[:, g * P:(g + 1) * P], condw_rep[:, g * P:(g + 1) * P], cond_t,
                                 start=True, stop=False)
                last = nc.tensor.matmul(ps_g[:, g * P:(g + 1) * P], fside_rep[:, g * P:(g + 1) * P], ones,
                                        start=False, stop=True)
            last.then_inc(x_transposed, 1)

            def chunk(u, par):
                transpose_x(u, par, 0, True)
                transpose_x(u, par, 1, True)
                if not (isinstance(u, int) and u == 0 and par == 0):
                    convolve(u + par - 1, 1 - par, 3, True)
                transpose_x(u, par, 2, True)
                convolve(u, par, 0, True)
                transpose_x(u, par, 3, True)
                transpose_w(u, par, 0)
                convolve(u, par, 1, True)
                transpose_x(u, par, 4, True)
                transpose_w(u, par, 1)
                convolve(u, par, 2, True)

            chunk(0, 0)
            chunk(0, 1)
            with pe.Fori(1, 4) as u:
                for par in range(2):
                    chunk(u, par)
            chunk(4, 0)
            chunk(4, 1)
            convolve(4, 1, 3, True)

            def tile(u, q, conv):
                p = q % 2
                v, par = u + AHEAD // 2, q // 2
                rounds, steps = half_of(q)
                hi, lo = yt_hi[p], yt_lo[p]
                if conv:
                    transpose_x(v, par, rounds[0], False)
                pe.wait_ge(y_lo, u * 4 + (q + 1))
                wait(pe, gh_ready, u * 4 + q)
                for t in range(PH):
                    for i, (a, b) in enumerate(((hi, ws_lo), (lo, ws_hi), (hi, ws_hi))):
                        last = nc.tensor.matmul(ps_s[:, 0:SIDE], a[:, t, :], b[:, t, :],
                                                start=(t == 0 and i == 0), stop=(t == PH - 1 and i == 2))
                last.then_inc(side_done, 1)
                if conv:
                    transpose_x(v, par, rounds[1], False)
                wait(pe, out_ready, u * 4 + (q - 1))

                def base(phases):
                    for t in phases:
                        for i, (a, b) in enumerate(((hi, wb_lo), (lo, wb_hi), (hi, wb_hi))):
                            for h in range(2):
                                nc.tensor.matmul(ps_b[p][:, h, :], a[:, t, :], b[:, t, h * BANK:(h + 1) * BANK],
                                                 start=(t == 0 and i == 0), stop=False)

                base((0, 1))
                if conv:
                    convolve(v, par, steps[0], False)
                    if len(rounds) == 3:
                        transpose_x(v, par, rounds[2], False)
                base((2, 3))
                if conv:
                    convolve(v, par, steps[1], False)
                base((4, 5))
                pe.wait_ge(gh_ready, u * 4 + (q + 1))
                wait(pe, g_lo, u * 4 + q)
                for h in range(2):
                    last = nc.tensor.transpose(ps_g[0:HALF, h * P:(h + 1) * P], gh[:, h * HALF:(h + 1) * HALF],
                                               ident[:, :])
                last.then_inc(g_transposed, 1)
                base((6, 7))
                if isinstance(u, int) and u == 0 and q == 0:
                    pe.wait_ge(bt_ready, 1)
                pe.wait_ge(g_lo, u * 4 + (q + 1))
                for k in range(2):
                    for i, (a, b) in enumerate(((gt_hi, bt_lo), (gt_lo, bt_hi), (gt_hi, bt_hi))):
                        for h in range(2):
                            last = nc.tensor.matmul(ps_b[p][:, h, :], a[:, k, :], b[:, k, h * BANK:(h + 1) * BANK],
                                                    start=False, stop=(k == 1 and i == 2))
                last.then_inc(base_done, 1)

            pe.wait_ge(y_evac, AHEAD * STEPS)
            pe.wait_ge(w_lo, W_ROUNDS * W_CHUNKS)
            for q in range(4):
                tile(0, q, True)
            with pe.Fori(1, 11) as u:
                for q in range(4):
                    tile(u, q, True)
            with pe.Fori(11, 16) as u:
                for q in range(4):
                    tile(u, q, False)

        @block.scalar
        def _(act):
            def pack(u, par, half):
                act.wait_ge(x_in[par], u * 32 + 32)
                if not (isinstance(u, int) and u == 0 and par == 0):
                    act.wait_ge(x_transposed, x_round(u, par, 0) - (0 if half else ROUNDS - 2))
                lo, hi = (0, 2 * STEP_BLOCKS) if half == 0 else (2 * STEP_BLOCKS, CHUNK_BLOCKS + 1)
                nc.scalar.activation(xp[:, lo:hi, :].rearrange("p b (c j) -> p b c j", j=PH),
                                     xs[par][:, :, lo * PH:hi * PH].rearrange("p c (b j) -> p b c j", j=PH),
                                     ACT.Copy).then_inc(x_packed[half], 1)

            def store_y(u, par, s):
                act.wait_ge(y_evac, step_number(u, par, s) + 1)
                group = u // 4
                first = (u % 4) * (2 * CHUNK_BLOCKS) + (par * CHUNK_BLOCKS + s * STEP_BLOCKS)
                dst = y_dram[bass.ds(group * GC, GC), :, bass.ds(first, STEP_BLOCKS), :]
                act.dma_start(dst.rearrange("o t b n -> (o t) (b n)"), y_st[:, s, :]).then_inc(y_out[s], 16)

            def store_out(u, q):
                act.wait_ge(out_ready, u * 4 + (q + 1))
                act.dma_start(out[:, u * 4 + q, :], res[:, q, :]).then_inc(out_done[q], 16)

            def split_x(u, par, k, both):
                act.wait_ge(x_transposed, x_round(u, par, k) + 1)
                blocks = round_blocks(k)
                bank = x_bank(par, k, both)
                nc.scalar.activation(xt_hi[:, blocks.start:blocks.stop, :].rearrange("p b n -> p (b n)"),
                                     bank[:, 0:len(blocks) * P], ACT.Copy).then_inc(x_hi, 1)

            def split_w(u, par, half):
                act.wait_ge(w_transposed, u * 4 + (par * 2 + half + 1))
                rows = w_columns(u, par)
                nc.scalar.activation(w_dest(u, par, half, True),
                                     w_bank[half][:, 0:4 * rows].rearrange("p (t n) -> p t n", t=4),
                                     ACT.Copy).then_inc(w_hi, 1)

            def split_y(u, q):
                p = q % 2
                act.wait_ge(y_in[p], u * 32 + (16 * (q // 2) + 16))
                wait(act, base_done, u * 4 + (q - 1))
                nc.scalar.activation(yt_hi[p][:, :, :].rearrange("p t n -> p (t n)"), y_raw[:, p, :],
                                     ACT.Copy).then_inc(y_hi, 1)

            for h in range(2):
                act.wait_ge(x_transposed, h + 2)
                nc.scalar.activation(toep_hi[:, :, h * P:(h + 1) * P].rearrange("p g (o t) -> p g o t", t=PH),
                                     x_banks[1 - h][:, :].rearrange("p (t g o) -> p g o t", t=PH, g=GROUPS),
                                     ACT.Copy).then_inc(x_hi, 1)

            def chunk(u, par):
                pending = not (isinstance(u, int) and u == 0 and par == 0)
                split_x(u, par, 0, True)
                split_x(u, par, 1, True)
                if pending:
                    store_y(u + par - 1, 1 - par, 2)
                pack(u + par, 1 - par, 0)
                split_x(u, par, 2, True)
                if pending:
                    store_y(u + par - 1, 1 - par, 3)
                split_x(u, par, 3, True)
                split_w(u, par, 0)
                store_y(u, par, 0)
                split_x(u, par, 4, True)
                split_w(u, par, 1)
                pack(u + par, 1 - par, 1)
                store_y(u, par, 1)

            pack(0, 0, 0)
            pack(0, 0, 1)
            chunk(0, 0)
            act.wait_ge(lora_in, 64)
            act.wait_ge(bias_ready, 1)
            nc.scalar.activation(lora_dei.rearrange("p (r o) -> p o r", r=RANK),
                                 lora_nat.rearrange("p (o r) -> p o r", r=RANK), ACT.Copy).then_inc(lora_dei_ready, 1)
            chunk(0, 1)
            with act.Fori(1, 4) as u:
                for par in range(2):
                    chunk(u, par)
            chunk(4, 0)
            chunk(4, 1)
            store_y(4, 1, 2)
            store_y(4, 1, 3)
            act.wait_ge(lora_raw_in, 16)
            nc.scalar.activation(bt_hi[:, :, :].rearrange("p h d -> p (h d)"), lora_raw,
                                 ACT.Copy).then_inc(bt_hi_ready, 1)

            def tile(u, q, conv, first=False, last=False, last_chunk=False):
                v, par = u + AHEAD // 2, q // 2
                rounds = half_of(q)[0]
                if conv:
                    split_x(v, par, rounds[0], False)
                    if q % 2 == 0 and not first:
                        store_y(v + par - 1, 1 - par, 3)
                    elif q % 2 == 1:
                        store_y(v, par, 1)
                if q > 0:
                    store_out(u, q - 1)
                elif not first:
                    store_out(u - 1, 3)
                if conv:
                    split_x(v, par, rounds[1], False)
                act.wait_ge(diff_ready, u * 4 + (q + 1))
                nc.scalar.activation(ed[:, :], diff[:, :], ACT.Exp).then_inc(exp_ready, 1)
                if conv and q % 2 == 0:
                    if not last_chunk:
                        pack(v + par, 1 - par, 0)
                    store_y(v, par, 0)
                    split_x(v, par, rounds[2], False)
                if not last:
                    split_y(u + (1 if q == 3 else 0), (q + 1) % 4)
                if conv and q % 2 == 1:
                    if not last_chunk:
                        pack(v + par, 1 - par, 1)
                    store_y(v, par, 2)
                act.wait_ge(g_transposed, u * 4 + (q + 1))
                nc.scalar.activation(gt_hi[:, :, :].rearrange("p h n -> p (h n)"), ps_g[0:HALF, 0:2 * P],
                                     ACT.Copy).then_inc(g_hi, 1)

            split_y(0, 0)
            for q in range(4):
                tile(0, q, True, first=(q == 0))
            with act.Fori(1, 10) as u:
                for q in range(4):
                    tile(u, q, True)
            for q in range(4):
                tile(10, q, True, last_chunk=(q >= 2))
            store_y(15, 1, 3)
            with act.Fori(11, 15) as u:
                for q in range(4):
                    tile(u, q, False)
            for q in range(4):
                tile(15, q, False, last=(q == 3))
            store_out(15, 3)
            for s in range(STEPS):
                act.wait_ge(y_out[s], 16 * GROUPS * CHUNKS_PER_GROUP)
            for q in range(4):
                act.wait_ge(out_done[q], 16 * TILES // 4)

        @block.vector
        def _(dve):
            def split_x(u, par, k, both):
                r = x_round(u, par, k)
                dve.wait_ge(x_hi, r - 1)
                blocks = round_blocks(k)
                bank = x_bank(par, k, both)
                cols = slice(blocks.start, blocks.stop)
                nc.vector.tensor_tensor(xt_lo[:, cols, :].rearrange("p b n -> p (b n)"),
                                        bank[:, 0:len(blocks) * P],
                                        xt_hi[:, cols, :].rearrange("p b n -> p (b n)").bitcast(F32),
                                        ALU.subtract).then_inc(x_lo, 1)

            def evacuate_conv(u, par, s, both):
                dve.wait_ge(conv_done, step_number(u, par, s) + 1)
                if s == 0:
                    dve.wait_ge(toep_ready, u * 6 + (par * 3 + 3))
                if not (isinstance(u, int) and u == 0 and par == 0):
                    wait(dve, y_out[s], u * 32 + par * 16)
                nc.vector.tensor_tensor(y_st[:, s, :].rearrange("p (b n) -> p b n", n=IMAGES),
                                        c_bank(s, both)[:, :].rearrange("p (b n) -> p b n", n=IMAGES),
                                        bias_cur[par][:, :].unsqueeze(1).to_broadcast([P, STEP_BLOCKS, IMAGES]),
                                        ALU.add).then_inc(y_evac, 1)

            def split_w(u, par, half):
                dve.wait_ge(w_hi, u * 4 + (par * 2 + half + 1))
                rows = w_columns(u, par)
                nc.vector.tensor_tensor(w_dest(u, par, half, False),
                                        w_bank[half][:, 0:4 * rows].rearrange("p (t n) -> p t n", t=4),
                                        w_dest(u, par, half, True).bitcast(F32), ALU.subtract).then_inc(w_lo, 1)

            def split_y(u, q):
                p = q % 2
                dve.wait_ge(y_hi, u * 4 + (q + 1))
                nc.vector.tensor_tensor(yt_lo[p][:, :, :].rearrange("p t n -> p (t n)"), y_raw[:, p, :],
                                        yt_hi[p][:, :, :].rearrange("p t n -> p (t n)").bitcast(F32),
                                        ALU.subtract).then_inc(y_lo, 1)

            dve.wait_ge(small_in, 64)
            dve.wait_ge(const_ready, 5)
            for t in range(PH):
                taps = conv_nat.rearrange("o (c k) -> o c k", k=TAPS)
                near = spread[:, t, 0, :].rearrange("o (c j) -> o c j", j=PH)
                far = spread[:, t, 1, :].rearrange("o (c j) -> o c j", j=PH)
                nc.vector.tensor_copy(near[:, :, t:PH], taps[:, :, 0:PH - t])
                ins = nc.vector.tensor_copy(far[:, :, 0:t + 1], taps[:, :, PH - t:TAPS])
            ins.then_inc(spread_ready, 1)
            nc.vector.tensor_copy(fside_rep.rearrange("p (o t) -> p o t", t=PH),
                                  fside_nat.unsqueeze(2).to_broadcast([1, CHANNELS, PH]))
            dve.wait_ge(x_transposed, 1)
            nc.vector.tensor_copy(cond_t, ps_x[:, 0:P])
            nc.vector.tensor_copy(condw_rep.rearrange("p (o t) -> p o t", t=PH),
                                  ps_x[:, P:P + CHANNELS].unsqueeze(2).to_broadcast([P, CHANNELS, PH])
                                  ).then_inc(x_lo, 1)
            nc.vector.engine_nop().then_inc(cond_ready, 1)
            for h in range(2):
                dve.wait_ge(x_hi, h + 1)
                cols = toep_hi[:, :, h * P:(h + 1) * P].rearrange("p g (o t) -> p g o t", t=PH)
                nc.vector.tensor_tensor(toep_lo[:, :, h * P:(h + 1) * P].rearrange("p g (o t) -> p g o t", t=PH),
                                        x_banks[1 - h][:, :].rearrange("p (t g o) -> p g o t", t=PH, g=GROUPS),
                                        cols.bitcast(F32), ALU.subtract).then_inc(x_lo, 1)
            nc.vector.engine_nop().then_inc(toep_made, 2)
            dve.wait_ge(x_transposed, PREP_ROUNDS)
            nc.vector.tensor_copy(bias[:, :, :].rearrange("p g n -> p (g n)"), ps_g[:, :]).then_inc(x_lo, 1)
            nc.vector.engine_nop().then_inc(bias_ready, 1)

            def chunk(u, par):
                split_x(u, par, 0, True)
                split_x(u, par, 1, True)
                if not (isinstance(u, int) and u == 0 and par == 0):
                    evacuate_conv(u + par - 1, 1 - par, 3, True)
                split_x(u, par, 2, True)
                evacuate_conv(u, par, 0, True)
                split_x(u, par, 3, True)
                split_w(u, par, 0)
                evacuate_conv(u, par, 1, True)
                split_x(u, par, 4, True)
                split_w(u, par, 1)
                evacuate_conv(u, par, 2, True)

            chunk(0, 0)
            chunk(0, 1)
            with dve.Fori(1, 4) as u:
                for par in range(2):
                    chunk(u, par)
            chunk(4, 0)
            chunk(4, 1)
            evacuate_conv(4, 1, 3, True)
            dve.wait_ge(bt_hi_ready, 1)
            nc.vector.tensor_tensor(bt_lo[:, :, :].rearrange("p h d -> p (h d)"), lora_raw,
                                    bt_hi[:, :, :].rearrange("p h d -> p (h d)").bitcast(F32),
                                    ALU.subtract).then_inc(bt_ready, 1)

            def add_residual(u, q):
                dve.wait_ge(base_done, u * 4 + (q + 1))
                dve.wait_ge(res_in[q], u * 16 + 16)
                nc.vector.tensor_tensor(res[:, q, :].rearrange("p (h d) -> p h d", h=2), ps_b[q % 2][:, :, :],
                                        res[:, q, :].rearrange("p (h d) -> p h d", h=2),
                                        ALU.add).then_inc(out_ready, 1)

            def tile(u, q, conv, first=False, last=False):
                v, par = u + AHEAD // 2, q // 2
                rounds, steps = half_of(q)
                at = (u * 4 + q) * GATE_STEPS
                if conv:
                    split_x(v, par, rounds[0], False)
                if q > 0:
                    add_residual(u, q - 1)
                elif not first:
                    add_residual(u - 1, 3)
                dve.wait_ge(side_done, u * 4 + (q + 1))
                stand_alone(dve)
                nc.vector.max(mx[:, :], ps_s[:, 0:EXPERTS]).then_inc(gate_step, 1)
                dve.wait_ge(gate_step, at + 1)
                nc.vector.tensor_tensor(diff[:, :], mx[:, 1:2], mx[:, 0:1], ALU.subtract).then_inc(diff_ready, 1)
                nc.vector.max_index(mi[:, :], mx[:, :], ps_s[:, 0:EXPERTS]).then_inc(gate_step, 1)
                dve.wait_ge(gate_step, at + 2)
                nc.vector.tensor_copy(mif[:, :], mi[:, 0:2]).then_inc(gate_step, 1)
                if conv:
                    split_x(v, par, rounds[1], False)
                dve.wait_ge(gate_step, at + 3)
                nc.vector.tensor_scalar(is0[:, :], iota[:, :], mif[:, 0:1], None, ALU.is_equal).then_inc(gate_step, 1)
                nc.vector.tensor_scalar(is1[:, :], iota[:, :], mif[:, 1:2], None, ALU.is_equal).then_inc(gate_step, 1)
                dve.wait_ge(exp_ready, u * 4 + (q + 1))
                nc.vector.tensor_scalar(den[:, :], ed[:, :], 1.0, 1.0 / SCALING, ALU.add, ALU.mult
                                        ).then_inc(gate_step, 1)
                dve.wait_ge(gate_step, at + 6)
                nc.vector.reciprocal(p0[:, :], den[:, :]).then_inc(gate_step, 1)
                nc.vector.scalar_tensor_tensor(out=gate[:, :], in0=is1[:, :], scalar=ed[:, 0:1], in1=is0[:, :],
                                               op0=ALU.mult, op1=ALU.add).then_inc(gate_step, 1)
                dve.wait_ge(gate_step, at + 8)
                wait(dve, g_transposed, u * 4 + q)
                nc.vector.scalar_tensor_tensor(
                    out=gh[:, :].rearrange("p (e r) -> p e r", r=RANK),
                    in0=ps_s[:, EXPERTS:SIDE].rearrange("p (e r) -> p e r", r=RANK), scalar=p0[:, 0:1],
                    in1=gate[:, :].unsqueeze(2).to_broadcast([P, EXPERTS, RANK]),
                    op0=ALU.mult, op1=ALU.mult).then_inc(gh_ready, 1)
                if conv:
                    evacuate_conv(v, par, steps[0], False)
                    if len(rounds) == 3:
                        split_x(v, par, rounds[2], False)
                if not last:
                    split_y(u + (1 if q == 3 else 0), (q + 1) % 4)
                if conv:
                    evacuate_conv(v, par, steps[1], False)
                dve.wait_ge(g_hi, u * 4 + (q + 1))
                nc.vector.tensor_tensor(gt_lo[:, :, :].rearrange("p h n -> p (h n)"), ps_g[0:HALF, 0:2 * P],
                                        gt_hi[:, :, :].rearrange("p h n -> p (h n)").bitcast(F32),
                                        ALU.subtract).then_inc(g_lo, 1)

            split_y(0, 0)
            for q in range(4):
                tile(0, q, True, q == 0)
            with dve.Fori(1, 11) as u:
                for q in range(4):
                    tile(u, q, True)
            with dve.Fori(11, 15) as u:
                for q in range(4):
                    tile(u, q, False)
            for q in range(4):
                tile(15, q, False, False, q == 3)
            add_residual(15, 3)


_INS = ["x", "cond_128", "fside_S_0", "L0_cond_weight", "L0_cond_c_weight", "L0_ffn_base_W", "L0_ffn_gate_W",
        "L0_ffn_lora_A", "L0_ffn_lora_B"]


def kernel(**inputs):
    import numpy as _np
    import concourse.bacc as _bacc
    from concourse.bass_utils import run_bass_kernel_spmd as _run

    nc = _bacc.Bacc("TRN2", target_bir_lowering=False, num_devices=1)
    arrays, args = {}, []
    for name in _INS:
        a = _np.ascontiguousarray(inputs[name])
        arrays[f"in_{name}"] = a
        args.append(nc.dram_tensor(f"in_{name}", a.shape, F32, kind="ExternalInput").ap())
    o = nc.dram_tensor("out_dram", (IMAGES, CHANNELS, D_OUT), F32, kind="ExternalOutput").ap()
    adaln_ffn(nc, *args, o)
    r = _run(nc, [arrays], core_ids=[0])
    return r.results[0]["out_dram"]
```

```python
from contextlib import ExitStack

import concourse.bass as bass
from concourse import mybir

F32 = mybir.dt.float32
F32R = mybir.dt.float32r
U32 = mybir.dt.uint32
ALU = mybir.AluOpType
ACT = mybir.ActivationFunctionType


P = 128
IMAGES = 128
CHANNELS = 64
LENGTH = 1024
GROUPS = 4
GC = CHANNELS // GROUPS
TAPS = 9
PAD = TAPS // 2
PH = P // GC
BLOCKS = LENGTH // PH
EXPERTS = 28
RANK = 8
HID = EXPERTS * RANK
SIDE = EXPERTS + HID
D_OUT = 1024
SCALING = 2.0
BANK = 512

CHUNK = 128
CHUNKS_PER_GROUP = LENGTH // CHUNK
SQ = 32
QUARTERS = P // SQ
QC = GC // QUARTERS
CHUNK_BLOCKS = CHUNK // PH
PAIR = 2 * CHUNK
PAIRS_PER_GROUP = LENGTH // PAIR
XCOLS = PAIR + 2 * PAD
STEP_BLOCKS = BANK // P
STEPS = CHUNK_BLOCKS // STEP_BLOCKS
ROUNDS = STEPS + 1
POOL_ROUNDS = (1, 2, 3)
BATCHES = (ROUNDS + 1) // 2
POOL_LOADS = (6, 6)
X_LOADS = QUARTERS * QC
HALF = HID // 2

TILES = CHANNELS
AHEAD = 10
GATE_STEPS = 8
W_ROUNDS = 2
W_CHUNKS = AHEAD


def adaln_ffn(nc, x, cond, fside, conv_w, cond_w, base_w, gate_w, lora_a, lora_b, out):
    y_dram = nc.dram_tensor("y_scratch", (CHANNELS, PH, BLOCKS, IMAGES), F32, kind="Internal").ap()
    bt_dram = nc.dram_tensor("lora_bt_scratch", (HID, D_OUT), F32, kind="Internal").ap()

    with ExitStack() as ctx:
        def sb(name, shape, dt=F32):
            return ctx.enter_context(nc.sbuf_tensor(name, shape, dt))

        def ps(name, shape):
            return ctx.enter_context(nc.psum_tensor(name, shape, F32))

        def sem(name):
            return ctx.enter_context(nc.semaphore(name))

        ident = sb("ident", [P, P])
        iota = sb("iota", [P, EXPERTS])
        wb_hi = sb("wb_hi", [P, PH, D_OUT], F32R)
        wb_lo = sb("wb_lo", [P, PH, D_OUT], F32R)
        ws_hi = sb("ws_hi", [P, PH, SIDE], F32R)
        ws_lo = sb("ws_lo", [P, PH, SIDE], F32R)
        bt_hi = sb("bt_hi", [HALF, 2, D_OUT], F32R)
        bt_lo = sb("bt_lo", [HALF, 2, D_OUT], F32R)
        toep_hi = sb("toep_hi", [P, GROUPS, 2 * P], F32R)
        toep_lo = sb("toep_lo", [P, GROUPS, 2 * P], F32R)
        bias = sb("bias", [P, GROUPS, IMAGES])
        tc_hi = [sb(f"toep_cur_hi{i}", [P, 2, P], F32R) for i in range(2)]
        tc_lo = [sb(f"toep_cur_lo{i}", [P, 2, P], F32R) for i in range(2)]
        bias_cur = [sb(f"bias_cur{i}", [P, IMAGES]) for i in range(2)]
        xt = sb("xt", [P, CHUNK_BLOCKS + 1, IMAGES])
        xt_hi = sb("xt_hi", [P, CHUNK_BLOCKS + 1, IMAGES], F32R)
        xt_lo = sb("xt_lo", [P, CHUNK_BLOCKS + 1, IMAGES], F32R)
        y_st = sb("y_store", [P, STEPS, STEP_BLOCKS * IMAGES])
        y_raw = sb("y_raw", [P, 2, PH * IMAGES])
        res = sb("res", [P, 4, D_OUT])
        mx = sb("mx", [P, 8])
        mi = sb("mi", [P, 8], U32)
        mif = sb("mif", [P, 2])
        diff = sb("diff", [P, 1])
        ed = sb("ed", [P, 1])
        den = sb("den", [P, 1])
        p0 = sb("p0", [P, 1])
        is0 = sb("is0", [P, EXPERTS])
        is1 = sb("is1", [P, EXPERTS])
        gate = sb("gate", [P, EXPERTS])
        gh = sb("gh", [P, HID])
        gt_hi = sb("gt_hi", [HALF, 2, P], F32R)
        gt_lo = sb("gt_lo", [HALF, 2, P], F32R)

        xs = [sb("x_pair0", [P, GC, XCOLS])]
        with nc.sbuf_tensor("x_pair1", [P, GC, XCOLS], F32) as x_pair1:
            xs.append(x_pair1)
        yt_hi = [sb(f"yt_hi{i}", [P, PH, IMAGES], F32R) for i in range(2)]
        yt_lo = [sb(f"yt_lo{i}", [P, PH, IMAGES], F32R) for i in range(2)]
        sb("x_pair1_rest", [P, GC * XCOLS - 4 * PH * IMAGES])

        ps_d = ps("ps_d", [P, BANK])
        ps_g = ps("ps_g", [P, BANK])
        ps_c = ps("ps_c", [P, BANK])
        ps_s = ps("ps_s", [P, BANK])
        ps_b = [ps(f"ps_b{i}", [P, 2, BANK]) for i in range(2)]
        w_bank = [ps_b[0][:, 0, :], ps_b[0][:, 1, :]]
        toep_bank = [ps_b[1][:, 0, :], ps_b[1][:, 1, :]]
        bias_bank = ps_b[1][:, 0, :]
        tile_banks = [ps_c, ps_d]
        early_banks = [ps_c, ps_d, ps_s, ps_g]

        w_row = [res[:, i, :] for i in range(2)]
        lora_nat = y_raw[0:4 * EXPERTS, :, :].rearrange("p a n -> p (a n)")
        lora_dei = res[0:4 * EXPERTS, 2:4, :].rearrange("p a n -> p (a n)")
        lora_raw = y_raw[0:HALF, :, :].rearrange("p a n -> p (a n)")
        spread = y_st[0:CHANNELS, :, :].rearrange("p s (a h m) -> p (s a) h m", a=2, h=2)
        prep = res[:, 2, :]
        conv_nat = prep[0:CHANNELS, 0:GC * TAPS]
        cond_nat = prep[:, 160:160 + P]
        condw_nat = prep[0:CHANNELS, 288:288 + P]
        fside_nat = prep[0:1, 416:416 + CHANNELS]
        ones = prep[0:1, 480:480 + P]
        cond_t = y_raw[:, 1, 0:P]
        condw_rep = y_raw[:, 0, 0:CHANNELS * PH]
        fside_rep = y_raw[0:1, 1, P:P + CHANNELS * PH]

        x_in = [sem(f"x_in{i}") for i in range(2)]
        x_in_pool = [sem(f"x_in_pool{i}") for i in range(2)]
        w_in = [sem(f"w_in{i}") for i in range(2)]
        small_in = sem("small_in")
        lora_in = sem("lora_in")
        lora_out = sem("lora_out")
        lora_raw_in = sem("lora_raw_in")
        y_out = [sem(f"y_out{i}") for i in range(STEPS // 2)]
        y_in = [sem(f"y_in{i}") for i in range(2)]
        res_in = [sem(f"res_in{i}") for i in range(4)]
        out_done = [sem(f"out_done{i}") for i in range(4)]
        const_ready = sem("const_ready")
        x_padded = [sem(f"x_padded{i}") for i in range(2)]
        zeroed = sem("zeroed")
        passed = sem("passed")
        spread_ready = sem("spread_ready")
        cond_transposed = sem("cond_transposed")
        cond_ready = sem("cond_ready")
        bias_made = sem("bias_made")
        toep_transposed = sem("toep_transposed")
        toep_hi_made = sem("toep_hi_made")
        bias_ready = sem("bias_ready")
        toep_made = sem("toep_made")
        toep_ready = sem("toep_ready")
        lora_dei_ready = sem("lora_dei_ready")
        bt_hi_ready = sem("bt_hi_ready")
        bt_ready = sem("bt_ready")
        x_transposed = sem("x_transposed")
        x_hi = sem("x_hi")
        x_lo = [sem("x_lo_vector"), sem("x_lo_pool")]
        w_transposed = sem("w_transposed")
        w_hi = sem("w_hi")
        w_lo = sem("w_lo")
        conv_done = sem("conv_done")
        y_evac = sem("y_evac")
        y_hi = sem("y_hi")
        y_lo = sem("y_lo")
        side_done = sem("side_done")
        gate_step = sem("gate_step")
        diff_ready = sem("diff_ready")
        exp_ready = sem("exp_ready")
        gh_ready = sem("gh_ready")
        g_transposed = sem("g_transposed")
        g_hi = sem("g_hi")
        g_lo = sem("g_lo")
        base_done = sem("base_done")
        out_ready = sem("out_ready")

        def wait(eng, s, value):
            if not isinstance(value, int) or value > 0:
                eng.wait_ge(s, value)

        def stand_alone(eng):
            eng.sem_inc(passed, 1)

        def x_round(u, par, k):
            return u * (2 * ROUNDS) + (par * ROUNDS + k)

        def step_number(u, par, s):
            return u * (2 * STEPS) + (par * STEPS + s)

        def x_lo_count(u, par, k):
            same = [r for r in range(ROUNDS) if (r in POOL_ROUNDS) == (k in POOL_ROUNDS)]
            return u * (2 * len(same)) + (par * len(same) + same.index(k) + 1)

        def transposed(u, par, k):
            return u * (2 * BATCHES) + (par * BATCHES + k // 2 + 1)

        def pair_buffer(u):
            return (u + 1) % 2 if isinstance(u, int) and u < AHEAD // 2 else 0

        def x_in_count(u):
            pairs = u // 2 + 1 if isinstance(u, int) and u < AHEAD // 2 else u - 2
            return 16 * (pairs * X_LOADS - POOL_LOADS[1 - pair_buffer(u)])

        def x_part(u, group, pair, part):
            m, c = part // QC, part % QC
            first, end = max(pair * PAIR - PAD, 0), min((pair + 1) * PAIR + PAD, LENGTH)
            shift = first - (pair * PAIR - PAD)
            src = x[m * SQ:(m + 1) * SQ, bass.ds(group * GC, GC), first:end]
            src = src.rearrange("r (a c) l -> a r c l", a=QUARTERS)[:, :, c, :]
            return xs[pair_buffer(u)][:, m * QC + c, shift:shift + end - first], src

        def round_blocks(k):
            return slice(k * STEP_BLOCKS, min((k + 1) * STEP_BLOCKS, CHUNK_BLOCKS + 1))

        def w_dest(u, par, half, hi):
            ph = slice(4 * half, 4 * half + 4)
            if isinstance(u, int) and 2 * u + par >= 8:
                wide, lo = (ws_hi if hi else ws_lo), par * (SIDE // 2)
                return wide[:, ph, lo:lo + SIDE // 2]
            wide = wb_hi if hi else wb_lo
            return wide[:, ph, bass.ds(u * (2 * P) + par * P, P)]

        def w_columns(u, par):
            return SIDE // 2 if isinstance(u, int) and 2 * u + par >= 8 else P

        def half_of(t):
            return ((0, 1, 2), (0, 1)) if t % 2 == 0 else ((3, 4), (2, 3))

        block = ctx.enter_context(nc.Block())

        @block.sync
        def _(sp):
            def load_x(u, group, pair, parts=range(X_LOADS)):
                before = u - 2 if isinstance(u, int) and u <= AHEAD // 2 else u - 1
                if not (isinstance(u, int) and u < 2):
                    sp.wait_ge(x_transposed, transposed(before, 1, ROUNDS - 1))
                for part in parts:
                    dst, src = x_part(u, group, pair, part)
                    sp.dma_start(dst, src).then_inc(x_in[pair_buffer(u)], 16)

            def load_w(u, par):
                if not (isinstance(u, int) and u == 0):
                    wait(sp, w_transposed, u * (2 * W_ROUNDS) + (par - 1) * W_ROUNDS)
                if isinstance(u, int) and 2 * u + par == 8:
                    n = SIDE // 2 - EXPERTS
                    sp.dma_start(w_row[0][0:EXPERTS, :], gate_w).then_inc(w_in[0], 16)
                    sp.dma_start(w_row[0][EXPERTS:SIDE // 2, :], lora_rows[0:n, :]).then_inc(w_in[0], 16)
                elif isinstance(u, int) and 2 * u + par == 9:
                    n = SIDE // 2 - EXPERTS
                    sp.dma_start(w_row[1][0:SIDE // 2, :], lora_rows[n:HID, :]).then_inc(w_in[1], 16)
                else:
                    sp.dma_start(w_row[par], base_w[bass.ds(u * (2 * P) + par * P, P), :]).then_inc(w_in[par], 16)

            def load_tile_y(u, q):
                if q == 0:
                    for h in range(2):
                        wait(sp, y_out[h], (u // 4 + 1) * (16 * CHUNKS_PER_GROUP))
                wait(sp, y_lo, u * 4 + (q - 1))
                sp.dma_start(y_raw[:, q % 2, :].rearrange("b (t n) -> b t n", t=PH),
                             y_dram[u * 4 + q].rearrange("t b n -> b t n")).then_inc(y_in[q % 2], 16)

            def load_tile_x(u, q):
                if not (isinstance(u, int) and u == 0):
                    wait(sp, out_done[q], u * 16)
                sp.dma_start(res[:, q, :], x[:, u * 4 + q, :]).then_inc(res_in[q], 16)

            lora_rows = lora_a.rearrange("e r d -> (e r) d")
            sp.dma_start(conv_nat, conv_w.rearrange("o c k -> o (c k)")).then_inc(small_in, 16)
            sp.dma_start(cond_nat, cond).then_inc(small_in, 16)
            sp.dma_start(condw_nat, cond_w).then_inc(small_in, 16)
            sp.dma_start(fside_nat, fside.rearrange("(a n) -> a n", a=1)).then_inc(small_in, 16)
            load_x(0, 0, 0, range(X_LOADS - POOL_LOADS[0]))
            load_w(0, 0)
            load_w(0, 1)
            load_x(1, 0, 1, range(X_LOADS - POOL_LOADS[1]))
            sp.wait_ge(bias_ready, 1)
            for k in range(4):
                sp.dma_start(lora_nat[k * EXPERTS:(k + 1) * EXPERTS, :],
                             lora_b[:, k * 256:(k + 1) * 256, :].rearrange("e o r -> e (o r)")).then_inc(lora_in, 16)
            for u in range(1, AHEAD // 2):
                load_w(u, 0)
                load_x(u + 1, (u + 1) // PAIRS_PER_GROUP, (u + 1) % PAIRS_PER_GROUP)
                load_w(u, 1)
                if u == 2:
                    sp.wait_ge(lora_out, 64)
                    sp.dma_start(lora_raw.rearrange("p (h d) -> p h d", h=2),
                                 bt_dram.rearrange("(h p) d -> p h d", h=2)).then_inc(lora_raw_in, 16)
            sp.wait_ge(bt_ready, 4)
            load_tile_y(0, 0)
            load_tile_y(0, 1)
            sp.wait_ge(w_transposed, W_ROUNDS * W_CHUNKS)

            def four_tiles(u, group=None, pair=None):
                for q in range(4):
                    if not (isinstance(u, int) and u == 0 and q < 2):
                        load_tile_y(u, q)
                    if q == 3 and group is not None:
                        load_x(u + AHEAD // 2 + 1, group, pair)
                    load_tile_x(u, q)

            for u in range(2):
                four_tiles(u, 1, u + 2)
            with sp.Fori(2, GROUPS) as group:
                for pair in range(PAIRS_PER_GROUP):
                    four_tiles(group * PAIRS_PER_GROUP + pair - (AHEAD // 2 + 1), group, pair)
            with sp.Fori(10, 16) as u:
                four_tiles(u)

        @block.gpsimd
        def _(pool):
            def fetch_group(group, par):
                if not isinstance(group, int):
                    wait(pool, y_evac, group * (CHUNKS_PER_GROUP * STEPS) + (par - 1) * STEPS)
                stand_alone(pool)
                pool.tensor_copy(tc_hi[par][:, :, :].rearrange("p a n -> p (a n)"),
                                 toep_hi[:, group, :].bitcast(F32)).then_inc(toep_ready, 1)
                pool.tensor_copy(tc_lo[par][:, :, :].rearrange("p a n -> p (a n)"),
                                 toep_lo[:, group, :].bitcast(F32)).then_inc(toep_ready, 1)
                pool.tensor_copy(bias_cur[par][:, :], bias[:, group, :]).then_inc(toep_ready, 1)

            pool.memset(ident[:, :], 0.0).then_inc(const_ready, 1)
            pool.wait_ge(const_ready, 1)
            pool.affine_select(out=ident[:, :], in_=ident[:, :], compare_op=ALU.not_equal, fill=1.0,
                               base=0, pattern=[[-1, P]], channel_multiplier=1).then_inc(const_ready, 1)
            pool.memset(ones, 1.0).then_inc(const_ready, 1)
            pool.iota(iota[:, :], pattern=[[1, EXPERTS]], base=0, channel_multiplier=0,
                      allow_small_or_imprecise_dtypes=True).then_inc(const_ready, 1)

            def split_x(u, par, k):
                pool.wait_ge(x_hi, x_round(u, par, k) + 1)
                if not isinstance(u, int):
                    stand_alone(pool)
                cols = round_blocks(k)
                pool.tensor_tensor(xt_lo[:, cols, :].rearrange("p b n -> p (b n)"),
                                   xt[:, cols, :].rearrange("p b n -> p (b n)"),
                                   xt_hi[:, cols, :].rearrange("p b n -> p (b n)").bitcast(F32),
                                   ALU.subtract).then_inc(x_lo[1], 1)

            def pad_x(u, end):
                if not (isinstance(u, int) and u == 0):
                    pool.wait_ge(x_transposed, transposed(u - 1, 1, ROUNDS - 1))
                if not isinstance(u, int):
                    stand_alone(pool)
                pad = slice(0, PAD) if end == 0 else slice(XCOLS - PAD, XCOLS)
                pool.memset(xs[pair_buffer(u)][:, :, pad], 0.0).then_inc(x_padded[end], 1)

            def pad_ahead(first, c):
                if c == CHUNKS_PER_GROUP - 2:
                    pad_x(first + PAIRS_PER_GROUP - 1, 1)
                elif c == CHUNKS_PER_GROUP - 1:
                    pad_x(first + PAIRS_PER_GROUP, 0)

            def split_lora_b(i):
                h, d = i // 2, slice((i % 2) * BANK, (i % 2 + 1) * BANK)
                pool.wait_ge(bt_hi_ready, 1)
                pool.tensor_tensor(bt_lo[:, h, d], lora_raw[:, i * BANK:(i + 1) * BANK],
                                   bt_hi[:, h, d].bitcast(F32), ALU.subtract).then_inc(bt_ready, 1)

            pad_x(0, 0)
            for u in range(2):
                for part in range(X_LOADS - POOL_LOADS[u], X_LOADS):
                    dst, src = x_part(u, 0, u, part)
                    pool.dma_start(dst, src).then_inc(x_in_pool[u], 16)
            pool.sem_inc(x_padded[1], 1)
            for k in POOL_ROUNDS:
                split_x(0, 0, k)
            pool.wait_ge(bias_ready, 1)
            fetch_group(0, 1)
            for c in range(1, CHUNKS_PER_GROUP):
                for k in POOL_ROUNDS:
                    split_x(c // 2, c % 2, k)
                    if k == 1:
                        pad_ahead(0, c)
                    elif c >= CHUNKS_PER_GROUP - 2:
                        split_lora_b((c % 2) * 2 + k - 2)
                if c <= 4:
                    pool.wait_ge(lora_dei_ready, 1)
                    pool.dma_start(bt_dram.rearrange("(e r) (k o) -> k e r o", r=RANK, k=4)[c - 1],
                                   lora_dei[(c - 1) * EXPERTS:c * EXPERTS, :].rearrange("e (r o) -> e r o", r=RANK)
                                   ).then_inc(lora_out, 16)
            with pool.Fori(1, GROUPS) as group:
                for c in range(CHUNKS_PER_GROUP):
                    if c < 2:
                        fetch_group(group, c)
                    pad_ahead(group * (CHUNKS_PER_GROUP // 2), c)
                    for k in POOL_ROUNDS:
                        split_x(group * (CHUNKS_PER_GROUP // 2) + c // 2, c % 2, k)

        @block.tensor
        def _(pe):
            def convolve(u, par, s, group, banks):
                if s == 0:
                    pe.wait_ge(toep_ready, 6 * group + 3 * par + 3)
                for k in (s, s + 1):
                    if s == 0 or k == s + 1:
                        pe.wait_ge(x_lo[k in POOL_ROUNDS], x_lo_count(u, par, k))
                n = step_number(u, par, s)
                wait(pe, y_evac, n + 1 - len(banks))
                bank = banks[s % len(banks)]
                passes = [(w, v, h) for h in range(2) for w, v in ((tc_lo, xt_hi), (tc_hi, xt_lo), (tc_hi, xt_hi))]
                for i, (w, v, h) in enumerate(passes):
                    b = s * STEP_BLOCKS + h
                    last = nc.tensor.matmul(bank[:, :], w[par][:, h, :], v[:, b:b + STEP_BLOCKS, :],
                                            start=(i == 0), stop=(i == len(passes) - 1))
                last.then_inc(conv_done, 1)

            def transpose_w(u, par, half):
                if half == 0:
                    if isinstance(u, int) and u == 4:
                        pe.wait_ge(w_in[par], 96 if par == 0 else 80)
                    else:
                        pe.wait_ge(w_in[par], u * 16 + 16)
                wait(pe, w_lo, u * 4 + (par * 2 + half - 1))
                rows = w_columns(u, par)
                for i in range(4):
                    ph = 4 * half + i
                    last = nc.tensor.transpose(w_bank[half][:, i * rows:(i + 1) * rows],
                                               w_row[par][0:rows, ph:D_OUT:PH], ident[0:rows, 0:rows])
                last.then_inc(w_transposed, 1)

            pe.wait_ge(small_in, 64)
            pe.wait_ge(const_ready, 4)
            nc.tensor.transpose(ps_s[:, 0:P], cond_nat, ident[:, :])
            nc.tensor.transpose(ps_s[:, P:P + CHANNELS], condw_nat,
                                ident[0:CHANNELS, 0:CHANNELS]).then_inc(cond_transposed, 1)
            pe.wait_ge(spread_ready, 1)
            for h in range(2):
                for t in range(PH):
                    last = nc.tensor.transpose(toep_bank[h][:, t * CHANNELS:(t + 1) * CHANNELS],
                                               spread[:, t, h, :], ident[0:CHANNELS, 0:CHANNELS])
                last.then_inc(toep_transposed, 1)

            def make_bias():
                pe.wait_ge(cond_ready, 3)
                pe.wait_ge(toep_made, 2)
                for g in range(GROUPS):
                    nc.tensor.matmul(bias_bank[:, g * P:(g + 1) * P], condw_rep[:, g * P:(g + 1) * P], cond_t,
                                     start=True, stop=False)
                    last = nc.tensor.matmul(bias_bank[:, g * P:(g + 1) * P], fside_rep[:, g * P:(g + 1) * P],
                                            ones, start=False, stop=True)
                last.then_inc(bias_made, 1)

            def chunk(u, par, group=0):
                if isinstance(u, int) and u == 0 and par == 0:
                    make_bias()
                else:
                    convolve(u + par - 1, 1 - par, 3, group, early_banks)
                convolve(u, par, 0, group, early_banks)
                transpose_w(u, par, 0)
                if isinstance(u, int) and 2 * u + par == AHEAD - 1:
                    transpose_w(u, par, 1)
                convolve(u, par, 1, group, early_banks)
                convolve(u, par, 2, group, early_banks)
                if not (isinstance(u, int) and 2 * u + par == AHEAD - 1):
                    transpose_w(u, par, 1)

            chunk(0, 0)
            chunk(0, 1)
            with pe.Fori(1, 4) as u:
                for par in range(2):
                    chunk(u, par)
            chunk(4, 0, 1)
            chunk(4, 1, 1)
            convolve(4, 1, 3, 1, early_banks)

            def tile(u, q, conv, group=None):
                p = q % 2
                v, par = u + AHEAD // 2, q // 2
                steps = half_of(q)[1]
                hi, lo = yt_hi[p], yt_lo[p]
                pe.wait_ge(y_lo, u * 4 + (q + 1))
                wait(pe, gh_ready, u * 4 + q)
                for t in range(PH):
                    for i, (a, b) in enumerate(((lo, ws_hi), (hi, ws_lo), (hi, ws_hi))):
                        last = nc.tensor.matmul(ps_s[:, 0:SIDE], a[:, t, :], b[:, t, :],
                                                start=(t == 0 and i == 0), stop=(t == PH - 1 and i == 2))
                last.then_inc(side_done, 1)
                wait(pe, out_ready, u * 4 + (q - 1))

                def base(phases):
                    for t in phases:
                        for i, (a, b) in enumerate(((lo, wb_hi), (hi, wb_lo), (hi, wb_hi))):
                            for h in range(2):
                                nc.tensor.matmul(ps_b[p][:, h, :], a[:, t, :], b[:, t, h * BANK:(h + 1) * BANK],
                                                 start=(t == 0 and i == 0), stop=False)

                base((0, 1, 2))
                if conv:
                    convolve(v, par, steps[0], group, tile_banks)
                base((3, 4))
                if conv:
                    convolve(v, par, steps[1], group, tile_banks)
                base((5,))
                pe.wait_ge(gh_ready, u * 4 + (q + 1))
                wait(pe, g_lo, u * 4 + q)
                for h in range(2):
                    last = nc.tensor.transpose(ps_g[0:HALF, h * P:(h + 1) * P], gh[:, h * HALF:(h + 1) * HALF],
                                               ident[:, :])
                last.then_inc(g_transposed, 1)
                base((6, 7))
                if isinstance(u, int) and u == 0 and q == 0:
                    pe.wait_ge(bt_ready, 1)
                pe.wait_ge(g_lo, u * 4 + (q + 1))
                for k in range(2):
                    for i, (a, b) in enumerate(((gt_lo, bt_hi), (gt_hi, bt_lo), (gt_hi, bt_hi))):
                        for h in range(2):
                            last = nc.tensor.matmul(ps_b[p][:, h, :], a[:, k, :], b[:, k, h * BANK:(h + 1) * BANK],
                                                    start=False, stop=(k == 1 and i == 2))
                last.then_inc(base_done, 1)

            pe.wait_ge(y_evac, AHEAD * STEPS)
            pe.wait_ge(w_lo, W_ROUNDS * W_CHUNKS)
            for q in range(4):
                tile(0, q, True, 1)
            for group, (first, end) in ((1, (1, 3)), (2, (3, 7)), (3, (7, 11))):
                with pe.Fori(first, end) as u:
                    for q in range(4):
                        tile(u, q, True, group)
            with pe.Fori(11, 16) as u:
                for q in range(4):
                    tile(u, q, False)

        @block.scalar
        def _(act):
            def store_y(u, par, h):
                act.wait_ge(y_evac, step_number(u, par, 2 * h + 1) + 1)
                group = u // 4
                first = (u % 4) * (2 * CHUNK_BLOCKS) + (par * CHUNK_BLOCKS + 2 * h * STEP_BLOCKS)
                dst = y_dram[bass.ds(group * GC, GC), :, bass.ds(first, 2 * STEP_BLOCKS), :]
                act.dma_start(dst.rearrange("o t b n -> (o t) (b n)"),
                              y_st[:, 2 * h:2 * h + 2, :].rearrange("p s n -> p (s n)")).then_inc(y_out[h], 16)

            def store_out(u, q):
                act.wait_ge(out_ready, u * 4 + (q + 1))
                act.dma_start(out[:, u * 4 + q, :], res[:, q, :]).then_inc(out_done[q], 16)

            def split_x(u, par, k):
                act.wait_ge(x_transposed, transposed(u, par, k))
                if not (isinstance(u, int) and u == 0 and par == 0):
                    act.wait_ge(conv_done, step_number(u, par, min(k, STEPS - 1)) + 1 - STEPS)
                cols = round_blocks(k)
                nc.scalar.activation(xt_hi[:, cols, :].rearrange("p b n -> p (b n)"),
                                     xt[:, cols, :].rearrange("p b n -> p (b n)"), ACT.Copy).then_inc(x_hi, 1)

            def split_w(u, par, half):
                act.wait_ge(w_transposed, u * 4 + (par * 2 + half + 1))
                rows = w_columns(u, par)
                nc.scalar.activation(w_dest(u, par, half, True),
                                     w_bank[half][:, 0:4 * rows].rearrange("p (t n) -> p t n", t=4),
                                     ACT.Copy).then_inc(w_hi, 1)

            def split_y(u, q):
                p = q % 2
                act.wait_ge(y_in[p], u * 32 + (16 * (q // 2) + 16))
                if isinstance(u, int) and u == 0 and q == 0:
                    act.wait_ge(x_transposed, transposed(AHEAD // 2 - 1, 1, ROUNDS - 1))
                wait(act, base_done, u * 4 + (q - 1))
                nc.scalar.activation(yt_hi[p][:, :, :].rearrange("p t n -> p (t n)"), y_raw[:, p, :],
                                     ACT.Copy).then_inc(y_hi, 1)

            for h in range(2):
                act.wait_ge(toep_transposed, h + 1)
                nc.scalar.activation(toep_hi[:, :, h * P:(h + 1) * P].rearrange("p g (o t) -> p g o t", t=PH),
                                     toep_bank[h].rearrange("p (t g o) -> p g o t", t=PH, g=GROUPS),
                                     ACT.Copy).then_inc(toep_hi_made, 1)

            def chunk(u, par):
                split_x(u, par, 3)
                split_x(u, par, 4)
                if not (isinstance(u, int) and u == 0 and par == 0):
                    store_y(u + par - 1, 1 - par, 1)
                split_w(u, par, 0)
                if isinstance(u, int) and 2 * u + par == AHEAD - 1:
                    split_w(u, par, 1)
                    split_y(0, 0)
                    store_y(u, par, 0)
                else:
                    split_x(u + par, 1 - par, 0)
                    store_y(u, par, 0)
                    split_w(u, par, 1)
                    split_x(u + par, 1 - par, 1)
                    split_x(u + par, 1 - par, 2)

            for k in range(3):
                split_x(0, 0, k)
            chunk(0, 0)
            act.wait_ge(lora_in, 64)
            act.wait_ge(bias_ready, 1)
            nc.scalar.activation(lora_dei.rearrange("p (r o) -> p o r", r=RANK),
                                 lora_nat.rearrange("p (o r) -> p o r", r=RANK), ACT.Copy).then_inc(lora_dei_ready, 1)
            chunk(0, 1)
            with act.Fori(1, 3) as u:
                for par in range(2):
                    chunk(u, par)
            act.wait_ge(lora_raw_in, 16)
            nc.scalar.activation(bt_hi[:, :, :].rearrange("p h d -> p (h d)"), lora_raw, ACT.Copy
                                 ).then_inc(bt_hi_ready, 1)
            chunk(3, 0)
            chunk(3, 1)
            chunk(4, 0)
            chunk(4, 1)
            store_y(4, 1, 1)

            def tile(u, q, conv, first=False, last=False):
                v, par = u + AHEAD // 2, q // 2
                rounds = half_of(q)[0]
                if conv:
                    split_x(v, par, rounds[0])
                    if q % 2 == 0 and not first:
                        store_y(v + par - 1, 1 - par, 1)
                    elif q % 2 == 1:
                        store_y(v, par, 0)
                if q > 0:
                    store_out(u, q - 1)
                elif not first:
                    store_out(u - 1, 3)
                if conv:
                    split_x(v, par, rounds[1])
                act.wait_ge(diff_ready, u * 4 + (q + 1))
                nc.scalar.activation(ed[:, :], diff[:, :], ACT.Exp).then_inc(exp_ready, 1)
                if conv and q % 2 == 0:
                    split_x(v, par, rounds[2])
                if not last:
                    split_y(u + (1 if q == 3 else 0), (q + 1) % 4)
                act.wait_ge(g_transposed, u * 4 + (q + 1))
                nc.scalar.activation(gt_hi[:, :, :].rearrange("p h n -> p (h n)"), ps_g[0:HALF, 0:2 * P],
                                     ACT.Copy).then_inc(g_hi, 1)

            for q in range(4):
                tile(0, q, True, first=(q == 0))
            with act.Fori(1, 11) as u:
                for q in range(4):
                    tile(u, q, True)
            store_y(15, 1, 1)
            with act.Fori(11, 15) as u:
                for q in range(4):
                    tile(u, q, False)
            for q in range(4):
                tile(15, q, False, last=(q == 3))
            store_out(15, 3)
            for h in range(2):
                act.wait_ge(y_out[h], 16 * GROUPS * CHUNKS_PER_GROUP)
            for q in range(4):
                act.wait_ge(out_done[q], 16 * TILES // 4)

        @block.vector
        def _(dve):
            def transpose_x(u, par, batch):
                if batch == 0:
                    if par == 0:
                        dve.wait_ge(x_padded[0], u // 4 + 1)
                        dve.wait_ge(x_in[pair_buffer(u)], x_in_count(u))
                        if isinstance(u, int) and u < 2:
                            dve.wait_ge(x_in_pool[u], 16 * POOL_LOADS[u])
                    else:
                        dve.wait_ge(x_padded[1], (u + 1) // 4 + 1)
                if not (isinstance(u, int) and u == 0 and par == 0):
                    for k in ((0, 1), (3,), (4,))[batch]:
                        by_pool = k in POOL_ROUNDS
                        rounds = len(POOL_ROUNDS) if by_pool else ROUNDS - len(POOL_ROUNDS)
                        dve.wait_ge(x_lo[by_pool], x_lo_count(u, par, k) - rounds)
                if not isinstance(u, int):
                    stand_alone(dve)
                first, end = 2 * batch * STEP_BLOCKS, min((batch + 1) * 2 * STEP_BLOCKS, CHUNK_BLOCKS + 1)
                src = xs[pair_buffer(u)][:, :, par * CHUNK + first * PH:par * CHUNK + end * PH]
                if end - first == 1:
                    last = nc.vector.transpose(xt[:, first, :].rearrange("p (m r) -> p m r", m=QUARTERS),
                                               src.rearrange("p (m c) j -> p m c j", m=QUARTERS))
                else:
                    for m in range(QUARTERS):
                        last = nc.vector.transpose(xt[:, first:end, m * SQ:(m + 1) * SQ],
                                                   src[:, m * QC:(m + 1) * QC, :].rearrange("p c (b j) -> p b c j", j=PH))
                last.then_inc(x_transposed, 1)

            def split_x(u, par, k):
                dve.wait_ge(x_hi, x_round(u, par, k) + 1)
                cols = round_blocks(k)
                nc.vector.tensor_tensor(xt_lo[:, cols, :].rearrange("p b n -> p (b n)"),
                                        xt[:, cols, :].rearrange("p b n -> p (b n)"),
                                        xt_hi[:, cols, :].rearrange("p b n -> p (b n)").bitcast(F32),
                                        ALU.subtract).then_inc(x_lo[0], 1)

            def evacuate_conv(u, par, s, banks):
                dve.wait_ge(conv_done, step_number(u, par, s) + 1)
                if s == 0:
                    dve.wait_ge(toep_ready, (u // 4) * 6 + (par * 3 + 3))
                if not (isinstance(u, int) and u == 0 and par == 0):
                    if s % 2 == 0:
                        wait(dve, y_out[s // 2], u * 32 + par * 16)
                nc.vector.tensor_tensor(y_st[:, s, :].rearrange("p (b n) -> p b n", n=IMAGES),
                                        banks[s % len(banks)][:, :].rearrange("p (b n) -> p b n", n=IMAGES),
                                        bias_cur[par][:, :].unsqueeze(1).to_broadcast([P, STEP_BLOCKS, IMAGES]),
                                        ALU.add).then_inc(y_evac, 1)

            def split_w(u, par, half):
                dve.wait_ge(w_hi, u * 4 + (par * 2 + half + 1))
                rows = w_columns(u, par)
                nc.vector.tensor_tensor(w_dest(u, par, half, False),
                                        w_bank[half][:, 0:4 * rows].rearrange("p (t n) -> p t n", t=4),
                                        w_dest(u, par, half, True).bitcast(F32), ALU.subtract).then_inc(w_lo, 1)

            def split_y(u, q):
                p = q % 2
                dve.wait_ge(y_hi, u * 4 + (q + 1))
                nc.vector.tensor_tensor(yt_lo[p][:, :, :].rearrange("p t n -> p (t n)"), y_raw[:, p, :],
                                        yt_hi[p][:, :, :].rearrange("p t n -> p (t n)").bitcast(F32),
                                        ALU.subtract).then_inc(y_lo, 1)

            nc.vector.memset(spread, 0.0).then_inc(zeroed, 1)
            dve.wait_ge(zeroed, 1)
            dve.wait_ge(small_in, 64)
            dve.wait_ge(const_ready, 4)
            for t in range(PH):
                taps = conv_nat.rearrange("o (c k) -> o c k", k=TAPS)
                near = spread[:, t, 0, :].rearrange("o (c j) -> o c j", j=PH)
                far = spread[:, t, 1, :].rearrange("o (c j) -> o c j", j=PH)
                nc.vector.tensor_copy(near[:, :, t:PH], taps[:, :, 0:PH - t])
                ins = nc.vector.tensor_copy(far[:, :, 0:t + 1], taps[:, :, PH - t:TAPS])
            ins.then_inc(spread_ready, 1)
            nc.vector.tensor_copy(fside_rep.rearrange("p (o t) -> p o t", t=PH),
                                  fside_nat.unsqueeze(2).to_broadcast([1, CHANNELS, PH])).then_inc(cond_ready, 1)
            dve.wait_ge(cond_transposed, 1)
            nc.vector.tensor_copy(cond_t, ps_s[:, 0:P]).then_inc(cond_ready, 1)
            nc.vector.tensor_copy(condw_rep.rearrange("p (o t) -> p o t", t=PH),
                                  ps_s[:, P:P + CHANNELS].unsqueeze(2).to_broadcast([P, CHANNELS, PH])
                                  ).then_inc(cond_ready, 1)
            for h in range(2):
                dve.wait_ge(toep_hi_made, h + 1)
                cols = toep_hi[:, :, h * P:(h + 1) * P].rearrange("p g (o t) -> p g o t", t=PH)
                nc.vector.tensor_tensor(toep_lo[:, :, h * P:(h + 1) * P].rearrange("p g (o t) -> p g o t", t=PH),
                                        toep_bank[h].rearrange("p (t g o) -> p g o t", t=PH, g=GROUPS),
                                        cols.bitcast(F32), ALU.subtract).then_inc(toep_made, 1)

            def first_group():
                dve.wait_ge(toep_made, 2)
                nc.vector.tensor_copy(tc_hi[0][:, :, :].rearrange("p a n -> p (a n)"),
                                      toep_hi[:, 0, :].bitcast(F32)).then_inc(toep_ready, 1)
                nc.vector.tensor_copy(tc_lo[0][:, :, :].rearrange("p a n -> p (a n)"),
                                      toep_lo[:, 0, :].bitcast(F32)).then_inc(toep_ready, 1)

            def evacuate_bias():
                dve.wait_ge(bias_made, 1)
                nc.vector.tensor_copy(bias_cur[0][:, :], bias_bank[:, 0:P]).then_inc(toep_ready, 1)
                nc.vector.tensor_copy(bias[:, :, :].rearrange("p g n -> p (g n)"), bias_bank).then_inc(bias_ready, 1)

            def chunk(u, par):
                then = (u + par, 1 - par)
                if u + par > 0:
                    evacuate_conv(u + par - 1, 1 - par, 3, early_banks)
                split_x(u, par, 4)
                if 2 * u + par < AHEAD - 1:
                    transpose_x(*then, 0)
                    evacuate_conv(u, par, 0, early_banks)
                    evacuate_conv(u, par, 1, early_banks)
                    split_w(u, par, 0)
                    transpose_x(*then, 1)
                    split_x(*then, 0)
                    transpose_x(*then, 2)
                    split_w(u, par, 1)
                    evacuate_conv(u, par, 2, early_banks)
                else:
                    evacuate_conv(u, par, 0, early_banks)
                    evacuate_conv(u, par, 1, early_banks)
                    split_w(u, par, 0)
                    split_w(u, par, 1)
                    split_y(0, 0)
                    evacuate_conv(u, par, 2, early_banks)

            first_group()
            for batch in range(BATCHES):
                transpose_x(0, 0, batch)
            split_x(0, 0, 0)
            evacuate_bias()
            for c in range(AHEAD):
                chunk(c // 2, c % 2)
            evacuate_conv(4, 1, 3, early_banks)
            for batch in range(BATCHES):
                transpose_x(AHEAD // 2, 0, batch)

            def add_residual(u, q):
                dve.wait_ge(base_done, u * 4 + (q + 1))
                dve.wait_ge(res_in[q], u * 16 + 16)
                nc.vector.tensor_tensor(res[:, q, :].rearrange("p (h d) -> p h d", h=2), ps_b[q % 2][:, :, :],
                                        res[:, q, :].rearrange("p (h d) -> p h d", h=2),
                                        ALU.add).then_inc(out_ready, 1)

            def tile(u, q, conv, first=False, last=False, last_chunk=False):
                v, par = u + AHEAD // 2, q // 2
                steps = half_of(q)[1]
                then = (v + par, 1 - par)
                at = (u * 4 + q) * GATE_STEPS
                if conv and q % 2 == 0:
                    split_x(v, par, 0)
                if q > 0:
                    add_residual(u, q - 1)
                elif not first:
                    add_residual(u - 1, 3)
                dve.wait_ge(side_done, u * 4 + (q + 1))
                stand_alone(dve)
                nc.vector.max(mx[:, :], ps_s[:, 0:EXPERTS]).then_inc(gate_step, 1)
                dve.wait_ge(gate_step, at + 1)
                nc.vector.tensor_tensor(diff[:, :], mx[:, 1:2], mx[:, 0:1], ALU.subtract).then_inc(diff_ready, 1)
                nc.vector.max_index(mi[:, :], mx[:, :], ps_s[:, 0:EXPERTS]).then_inc(gate_step, 1)
                dve.wait_ge(gate_step, at + 2)
                nc.vector.tensor_copy(mif[:, :], mi[:, 0:2]).then_inc(gate_step, 1)
                if conv and q % 2 == 1:
                    split_x(v, par, 4)
                if conv and q == 3 and not last_chunk:
                    transpose_x(*then, 0)
                dve.wait_ge(gate_step, at + 3)
                nc.vector.tensor_scalar(is0[:, :], iota[:, :], mif[:, 0:1], None, ALU.is_equal).then_inc(gate_step, 1)
                nc.vector.tensor_scalar(is1[:, :], iota[:, :], mif[:, 1:2], None, ALU.is_equal).then_inc(gate_step, 1)
                dve.wait_ge(exp_ready, u * 4 + (q + 1))
                nc.vector.tensor_scalar(den[:, :], ed[:, :], 1.0, 1.0 / SCALING, ALU.add, ALU.mult
                                        ).then_inc(gate_step, 1)
                dve.wait_ge(gate_step, at + 6)
                nc.vector.reciprocal(p0[:, :], den[:, :]).then_inc(gate_step, 1)
                nc.vector.scalar_tensor_tensor(out=gate[:, :], in0=is1[:, :], scalar=ed[:, 0:1], in1=is0[:, :],
                                               op0=ALU.mult, op1=ALU.add).then_inc(gate_step, 1)
                dve.wait_ge(gate_step, at + 8)
                wait(dve, g_transposed, u * 4 + q)
                nc.vector.scalar_tensor_tensor(
                    out=gh[:, :].rearrange("p (e r) -> p e r", r=RANK),
                    in0=ps_s[:, EXPERTS:SIDE].rearrange("p (e r) -> p e r", r=RANK), scalar=p0[:, 0:1],
                    in1=gate[:, :].unsqueeze(2).to_broadcast([P, EXPERTS, RANK]),
                    op0=ALU.mult, op1=ALU.mult).then_inc(gh_ready, 1)
                if conv:
                    evacuate_conv(v, par, steps[0], tile_banks)
                if not last:
                    split_y(u + (1 if q == 3 else 0), (q + 1) % 4)
                if conv:
                    if not last_chunk:
                        for batch in ((0,), (1, 2), (), (1, 2))[q]:
                            transpose_x(*then, batch)
                    evacuate_conv(v, par, steps[1], tile_banks)
                dve.wait_ge(g_hi, u * 4 + (q + 1))
                nc.vector.tensor_tensor(gt_lo[:, :, :].rearrange("p h n -> p (h n)"), ps_g[0:HALF, 0:2 * P],
                                        gt_hi[:, :, :].rearrange("p h n -> p (h n)").bitcast(F32),
                                        ALU.subtract).then_inc(g_lo, 1)

            for q in range(4):
                tile(0, q, True, q == 0)
            with dve.Fori(1, 10) as u:
                for q in range(4):
                    tile(u, q, True)
            for q in range(4):
                tile(10, q, True, last_chunk=(q >= 2))
            with dve.Fori(11, 15) as u:
                for q in range(4):
                    tile(u, q, False)
            for q in range(4):
                tile(15, q, False, False, q == 3)
            add_residual(15, 3)


_INS = ["x", "cond_128", "fside_S_0", "L0_cond_weight", "L0_cond_c_weight", "L0_ffn_base_W", "L0_ffn_gate_W",
        "L0_ffn_lora_A", "L0_ffn_lora_B"]


def kernel(**inputs):
    import numpy as _np
    import concourse.bacc as _bacc
    from concourse.bass_utils import run_bass_kernel_spmd as _run

    nc = _bacc.Bacc("TRN2", target_bir_lowering=False, num_devices=1)
    arrays, args = {}, []
    for name in _INS:
        a = _np.ascontiguousarray(inputs[name])
        arrays[f"in_{name}"] = a
        args.append(nc.dram_tensor(f"in_{name}", a.shape, F32, kind="ExternalInput").ap())
    o = nc.dram_tensor("out_dram", (IMAGES, CHANNELS, D_OUT), F32, kind="ExternalOutput").ap()
    adaln_ffn(nc, *args, o)
    r = _run(nc, [arrays], core_ids=[0])
    return r.results[0]["out_dram"]
```
